# Optimizing a Trainium2 kernel written in Bass

```python
import numpy as np
import jax
import jax.numpy as jnp

def _softmax(x, axis=-1):
    return jax.nn.softmax(x, axis=axis)

def _gelu(x):
    return jax.nn.gelu(x, approximate=True)

def _silu(x):
    return jax.nn.silu(x)

def _sigmoid(x):
    return jax.nn.sigmoid(x)

def _layernorm(x, axis=-1, eps=1e-05):
    m = jnp.mean(x, axis=axis, keepdims=True)
    v = jnp.var(x, axis=axis, keepdims=True)
    return (x - m) / jnp.sqrt(v + eps)

def _scatter_add(tgt, idx, src, axis=0):
    return tgt.at[idx].add(src)

def _segment_sum(src, seg, n):
    return jax.ops.segment_sum(src, seg, n)
kernel_name = 'mk_dlrm_tower_d1_rec_r8_908604'

def setup_inputs(seed: int=0):
    np.random.seed(seed)
    _w = jnp.asarray

    def _rec_inputs():
        import jax
        import jax.numpy as jnp
        _tk = jax.random.key(seed)
        dense_ctx = jax.random.normal(jax.random.fold_in(_tk, 190), (512, 16), jnp.float32)
        ids = jnp.stack([jax.random.randint(jax.random.fold_in(_tk, 200 + f), (512,), 0, v, jnp.int32) for f, v in enumerate([12500, 12500, 12500, 1250, 1000, 125000, 12500, 125000, 125000, 12500, 1000, 12500, 125000, 1250, 1250, 1000, 1250, 125000, 12500, 12500, 12500, 12500, 1250, 1000, 1000, 12500, 125000, 1000, 1250, 1250, 1000, 12500, 1250, 1000, 1250, 1250, 1000, 1250, 12500])], axis=1)
        tbl_0 = 0.05 * jax.random.normal(jax.random.fold_in(_tk, 500 + 0), (12500, 32), jnp.float32)
        tbl_1 = 0.05 * jax.random.normal(jax.random.fold_in(_tk, 500 + 1), (12500, 32), jnp.float32)
        tbl_2 = 0.05 * jax.random.normal(jax.random.fold_in(_tk, 500 + 2), (12500, 32), jnp.float32)
        tbl_3 = 0.05 * jax.random.normal(jax.random.fold_in(_tk, 500 + 3), (1250, 32), jnp.float32)
        tbl_4 = 0.05 * jax.random.normal(jax.random.fold_in(_tk, 500 + 4), (1000, 32), jnp.float32)
        tbl_5 = 0.05 * jax.random.normal(jax.random.fold_in(_tk, 500 + 5), (125000, 32), jnp.float32)
        tbl_6 = 0.05 * jax.random.normal(jax.random.fold_in(_tk, 500 + 6), (12500, 32), jnp.float32)
        tbl_7 = 0.05 * jax.random.normal(jax.random.fold_in(_tk, 500 + 7), (125000, 32), jnp.float32)
        tbl_8 = 0.05 * jax.random.normal(jax.random.fold_in(_tk, 500 + 8), (125000, 32), jnp.float32)
        tbl_9 = 0.05 * jax.random.normal(jax.random.fold_in(_tk, 500 + 9), (12500, 32), jnp.float32)
        tbl_10 = 0.05 * jax.random.normal(jax.random.fold_in(_tk, 500 + 10), (1000, 32), jnp.float32)
        tbl_11 = 0.05 * jax.random.normal(jax.random.fold_in(_tk, 500 + 11), (12500, 32), jnp.float32)
        tbl_12 = 0.05 * jax.random.normal(jax.random.fold_in(_tk, 500 + 12), (125000, 32), jnp.float32)
        tbl_13 = 0.05 * jax.random.normal(jax.random.fold_in(_tk, 500 + 13), (1250, 32), jnp.float32)
        tbl_14 = 0.05 * jax.random.normal(jax.random.fold_in(_tk, 500 + 14), (1250, 32), jnp.float32)
        tbl_15 = 0.05 * jax.random.normal(jax.random.fold_in(_tk, 500 + 15), (1000, 32), jnp.float32)
        tbl_16 = 0.05 * jax.random.normal(jax.random.fold_in(_tk, 500 + 16), (1250, 32), jnp.float32)
        tbl_17 = 0.05 * jax.random.normal(jax.random.fold_in(_tk, 500 + 17), (125000, 32), jnp.float32)
        tbl_18 = 0.05 * jax.random.normal(jax.random.fold_in(_tk, 500 + 18), (12500, 32), jnp.float32)
        tbl_19 = 0.05 * jax.random.normal(jax.random.fold_in(_tk, 500 + 19), (12500, 32), jnp.float32)
        tbl_20 = 0.05 * jax.random.normal(jax.random.fold_in(_tk, 500 + 20), (12500, 32), jnp.float32)
        tbl_21 = 0.05 * jax.random.normal(jax.random.fold_in(_tk, 500 + 21), (12500, 32), jnp.float32)
        tbl_22 = 0.05 * jax.random.normal(jax.random.fold_in(_tk, 500 + 22), (1250, 32), jnp.float32)
        tbl_23 = 0.05 * jax.random.normal(jax.random.fold_in(_tk, 500 + 23), (1000, 32), jnp.float32)
        tbl_24 = 0.05 * jax.random.normal(jax.random.fold_in(_tk, 500 + 24), (1000, 32), jnp.float32)
        tbl_25 = 0.05 * jax.random.normal(jax.random.fold_in(_tk, 500 + 25), (12500, 32), jnp.float32)
        tbl_26 = 0.05 * jax.random.normal(jax.random.fold_in(_tk, 500 + 26), (125000, 32), jnp.float32)
        tbl_27 = 0.05 * jax.random.normal(jax.random.fold_in(_tk, 500 + 27), (1000, 32), jnp.float32)
        tbl_28 = 0.05 * jax.random.normal(jax.random.fold_in(_tk, 500 + 28), (1250, 32), jnp.float32)
        tbl_29 = 0.05 * jax.random.normal(jax.random.fold_in(_tk, 500 + 29), (1250, 32), jnp.float32)
        tbl_30 = 0.05 * jax.random.normal(jax.random.fold_in(_tk, 500 + 30), (1000, 32), jnp.float32)
        tbl_31 = 0.05 * jax.random.normal(jax.random.fold_in(_tk, 500 + 31), (12500, 32), jnp.float32)
        tbl_32 = 0.05 * jax.random.normal(jax.random.fold_in(_tk, 500 + 32), (1250, 32), jnp.float32)
        tbl_33 = 0.05 * jax.random.normal(jax.random.fold_in(_tk, 500 + 33), (1000, 32), jnp.float32)
        tbl_34 = 0.05 * jax.random.normal(jax.random.fold_in(_tk, 500 + 34), (1250, 32), jnp.float32)
        tbl_35 = 0.05 * jax.random.normal(jax.random.fold_in(_tk, 500 + 35), (1250, 32), jnp.float32)
        tbl_36 = 0.05 * jax.random.normal(jax.random.fold_in(_tk, 500 + 36), (1000, 32), jnp.float32)
        tbl_37 = 0.05 * jax.random.normal(jax.random.fold_in(_tk, 500 + 37), (1250, 32), jnp.float32)
        tbl_38 = 0.05 * jax.random.normal(jax.random.fold_in(_tk, 500 + 38), (12500, 32), jnp.float32)
        _rk = jax.random.fold_in(_tk, 7)
        W_top1 = 0.0693375 * jax.random.normal(jax.random.fold_in(_tk, 801), (208, 512), jnp.float32)
        W_top2 = 0.0441942 * jax.random.normal(jax.random.fold_in(_tk, 802), (512, 256), jnp.float32)
        W_top3 = 0.0625 * jax.random.normal(jax.random.fold_in(_tk, 803), (256, 1), jnp.float32)
        b_top1 = jnp.zeros((512,), jnp.float32)
        b_top2 = jnp.zeros((256,), jnp.float32)
        return (dense_ctx, ids, tbl_0, tbl_1, tbl_2, tbl_3, tbl_4, tbl_5, tbl_6, tbl_7, tbl_8, tbl_9, tbl_10, tbl_11, tbl_12, tbl_13, tbl_14, tbl_15, tbl_16, tbl_17, tbl_18, tbl_19, tbl_20, tbl_21, tbl_22, tbl_23, tbl_24, tbl_25, tbl_26, tbl_27, tbl_28, tbl_29, tbl_30, tbl_31, tbl_32, tbl_33, tbl_34, tbl_35, tbl_36, tbl_37, tbl_38, W_top1, b_top1, W_top2, b_top2, W_top3)
    dense_ctx, ids, tbl_0, tbl_1, tbl_2, tbl_3, tbl_4, tbl_5, tbl_6, tbl_7, tbl_8, tbl_9, tbl_10, tbl_11, tbl_12, tbl_13, tbl_14, tbl_15, tbl_16, tbl_17, tbl_18, tbl_19, tbl_20, tbl_21, tbl_22, tbl_23, tbl_24, tbl_25, tbl_26, tbl_27, tbl_28, tbl_29, tbl_30, tbl_31, tbl_32, tbl_33, tbl_34, tbl_35, tbl_36, tbl_37, tbl_38, W_top1, b_top1, W_top2, b_top2, W_top3 = _rec_inputs()

    def _L0_rec_setup():
        import jax, jax.numpy as jnp
        import numpy as np
        LAYER_SIZES = (128, 128)

        def _cin_layer(h0, h, W):
            F0, Fi = (h0.shape[1], h.shape[1])
            K = W.shape[1]
            Wr = W.reshape(F0, Fi, K)
            return jnp.einsum('bid,bjd,ijk->bkd', h0, h, Wr)
        key = jax.random.key(seed)
        k1, k2, k3 = jax.random.split(key, 3)
        B, F0, D = (256, 39, 32)
        F1 = LAYER_SIZES[0] // 2
        x = jax.random.normal(k1, (B, F0, D), dtype=jnp.float32)
        W1 = jax.random.normal(k2, (F0 * F0, LAYER_SIZES[0]), dtype=jnp.float32) * 0.05
        W2 = jax.random.normal(k3, (F0 * F1, LAYER_SIZES[1]), dtype=jnp.float32) * 0.05
        return {'x': x, 'W1': W1, 'W2': W2}
    _L0_rec_all = _L0_rec_setup()
    _L0_rec_in = {k: v for k, v in _L0_rec_all.items() if k in ('W1', 'W2')}
    del _L0_rec_all
    return {'dense_ctx': dense_ctx, 'ids': ids, 'tbl_0': tbl_0, 'tbl_1': tbl_1, 'tbl_2': tbl_2, 'tbl_3': tbl_3, 'tbl_4': tbl_4, 'tbl_5': tbl_5, 'tbl_6': tbl_6, 'tbl_7': tbl_7, 'tbl_8': tbl_8, 'tbl_9': tbl_9, 'tbl_10': tbl_10, 'tbl_11': tbl_11, 'tbl_12': tbl_12, 'tbl_13': tbl_13, 'tbl_14': tbl_14, 'tbl_15': tbl_15, 'tbl_16': tbl_16, 'tbl_17': tbl_17, 'tbl_18': tbl_18, 'tbl_19': tbl_19, 'tbl_20': tbl_20, 'tbl_21': tbl_21, 'tbl_22': tbl_22, 'tbl_23': tbl_23, 'tbl_24': tbl_24, 'tbl_25': tbl_25, 'tbl_26': tbl_26, 'tbl_27': tbl_27, 'tbl_28': tbl_28, 'tbl_29': tbl_29, 'tbl_30': tbl_30, 'tbl_31': tbl_31, 'tbl_32': tbl_32, 'tbl_33': tbl_33, 'tbl_34': tbl_34, 'tbl_35': tbl_35, 'tbl_36': tbl_36, 'tbl_37': tbl_37, 'tbl_38': tbl_38, 'W_top1': W_top1, 'b_top1': b_top1, 'W_top2': W_top2, 'b_top2': b_top2, 'W_top3': W_top3, 'L0_rec_W1': _L0_rec_in['W1'], 'L0_rec_W2': _L0_rec_in['W2']}

def reference(dense_ctx, ids, tbl_0, tbl_1, tbl_2, tbl_3, tbl_4, tbl_5, tbl_6, tbl_7, tbl_8, tbl_9, tbl_10, tbl_11, tbl_12, tbl_13, tbl_14, tbl_15, tbl_16, tbl_17, tbl_18, tbl_19, tbl_20, tbl_21, tbl_22, tbl_23, tbl_24, tbl_25, tbl_26, tbl_27, tbl_28, tbl_29, tbl_30, tbl_31, tbl_32, tbl_33, tbl_34, tbl_35, tbl_36, tbl_37, tbl_38, W_top1, b_top1, W_top2, b_top2, W_top3, L0_rec_W1, L0_rec_W2):
    import jax
    import jax.numpy as jnp

    def _L0_rec_ref(x, W1, W2):
        import jax, jax.numpy as jnp
        import numpy as np
        LAYER_SIZES = (128, 128)

        def _cin_layer(h0, h, W):
            F0, Fi = (h0.shape[1], h.shape[1])
            K = W.shape[1]
            Wr = W.reshape(F0, Fi, K)
            return jnp.einsum('bid,bjd,ijk->bkd', h0, h, Wr)
        conv1 = _cin_layer(x, x, W1)
        half = LAYER_SIZES[0] // 2
        hidden1 = conv1[:, :half, :]
        final1 = conv1[:, half:, :]
        conv2 = _cin_layer(x, hidden1, W2)
        final = jnp.concatenate([final1, conv2], axis=1)
        return jnp.sum(final, axis=2)
    e = jnp.stack([tbl_0[ids[:, 0]], tbl_1[ids[:, 1]], tbl_2[ids[:, 2]], tbl_3[ids[:, 3]], tbl_4[ids[:, 4]], tbl_5[ids[:, 5]], tbl_6[ids[:, 6]], tbl_7[ids[:, 7]], tbl_8[ids[:, 8]], tbl_9[ids[:, 9]], tbl_10[ids[:, 10]], tbl_11[ids[:, 11]], tbl_12[ids[:, 12]], tbl_13[ids[:, 13]], tbl_14[ids[:, 14]], tbl_15[ids[:, 15]], tbl_16[ids[:, 16]], tbl_17[ids[:, 17]], tbl_18[ids[:, 18]], tbl_19[ids[:, 19]], tbl_20[ids[:, 20]], tbl_21[ids[:, 21]], tbl_22[ids[:, 22]], tbl_23[ids[:, 23]], tbl_24[ids[:, 24]], tbl_25[ids[:, 25]], tbl_26[ids[:, 26]], tbl_27[ids[:, 27]], tbl_28[ids[:, 28]], tbl_29[ids[:, 29]], tbl_30[ids[:, 30]], tbl_31[ids[:, 31]], tbl_32[ids[:, 32]], tbl_33[ids[:, 33]], tbl_34[ids[:, 34]], tbl_35[ids[:, 35]], tbl_36[ids[:, 36]], tbl_37[ids[:, 37]], tbl_38[ids[:, 38]]], axis=1)
    z = _L0_rec_ref(e, L0_rec_W1, L0_rec_W2)
    z = z.reshape(z.shape[0], -1)
    h = jnp.concatenate([z, dense_ctx], axis=1)
    h = jnp.maximum(h @ W_top1 + b_top1, 0.0)
    h = jnp.maximum(h @ W_top2 + b_top2, 0.0)
    y = h @ W_top3
    return y

_drawn_inputs = setup_inputs


def setup_inputs(seed=0):
    import zlib

    import numpy as np

    out = dict(_drawn_inputs(seed))
    spreads = {'b_top1': (0.0, 0.1), 'b_top2': (0.0, 0.1)}
    factors = {'tbl_0': 4.875,
     'tbl_1': 4.931,
     'tbl_2': 5.408,
     'tbl_3': 4.937,
     'tbl_4': 4.833,
     'tbl_5': 4.588,
     'tbl_6': 4.745,
     'tbl_7': 4.644,
     'tbl_8': 5.16,
     'tbl_9': 5.109,
     'tbl_10': 4.919,
     'tbl_11': 4.58,
     'tbl_12': 5.349,
     'tbl_13': 4.933,
     'tbl_14': 4.433,
     'tbl_15': 5.004,
     'tbl_16': 4.495,
     'tbl_17': 4.567,
     'tbl_18': 4.929,
     'tbl_19': 5.059,
     'tbl_20': 4.818,
     'tbl_21': 4.995,
     'tbl_22': 5.001,
     'tbl_23': 5.078,
     'tbl_24': 4.75,
     'tbl_25': 5.094,
     'tbl_26': 5.139,
     'tbl_27': 4.912,
     'tbl_28': 4.972,
     'tbl_29': 4.876,
     'tbl_30': 4.404,
     'tbl_31': 4.777,
     'tbl_32': 4.953,
     'tbl_33': 4.751,
     'tbl_34': 4.815,
     'tbl_35': 4.84,
     'tbl_36': 5.036,
     'tbl_37': 4.761,
     'tbl_38': 4.556,
     'L0_rec_W2': 5.624}
    for name, (base, spread) in spreads.items():
        noise = np.random.default_rng([zlib.crc32(name.encode()), seed]).standard_normal(out[name].shape)
        drawn = base * np.exp(spread * noise) if base else spread * noise
        out[name] = jnp.asarray(drawn.astype(out[name].dtype))
    for name, factor in factors.items():
        out[name] = (out[name] * factor).astype(out[name].dtype)
    return out
```

```python
from contextlib import ExitStack

import numpy as np
import concourse.bass as bass
from concourse import mybir

F32 = mybir.dt.float32
BF16 = mybir.dt.bfloat16
I32 = mybir.dt.int32
U32 = mybir.dt.uint32
ALU = mybir.AluOpType
ACT = mybir.ActivationFunctionType

P = 128
B = 512
F = 39
D = 32
K1 = 128
J = K1 // 2
K2 = 128
DENSE = 16
GROUPS = B // P
PAIRS = 4
COLS = P * D // PAIRS
CH = COLS // 2
QUADS = COLS // P
QB = P // D
SHIFTS = F // 2 + 1
PER_TILE = P // F
TILES = -(-SHIFTS // PER_TILE)
ROWS = [F * min(PER_TILE, SHIFTS - PER_TILE * t) for t in range(TILES)]
X3 = 3 * F
PIECES = 3
FP = F // PIECES
M1, M2 = 512, 256
HX = J + F
NZ = 4
ROUNDS = [(0, 3), (3, 6), (6, 8)]
TB = 8


def field_choices():
    m = np.zeros((3, F, 1 + TILES, PER_TILE, F), np.float32)
    for i in range(F):
        for r in range(PER_TILE):
            m[:, i, 0, r, i] = 1
            for t in range(TILES):
                if PER_TILE * t + r < SHIFTS:
                    m[:, (i + PER_TILE * t + r) % F, 1 + t, r, i] = 1
    return m.reshape(X3, (1 + TILES) * X3)


def pair_rows(s):
    n = F - s
    runs = [((0, n, s), (0, n, F * s))]
    if s:
        runs.append(((n, s, (F + 1) * n + s - F), (n, s, (F + 1) * n + F * (s - F))))
    return runs


def dlrm_tower(nc, dense, ids, tables, w_top1, b_top1, w_top2, b_top2, w_top3, w1, w2,
               choices, ident, ident16, out):
    with ExitStack() as ctx:
        def sb(name, shape, dt=F32):
            return ctx.enter_context(nc.sbuf_tensor(name, shape, dt))

        def sem(name):
            return ctx.enter_context(nc.semaphore(name))

        slots = ctx.enter_context(nc.psum_tensor("slots", [P, 2, COLS], F32))
        ps_h = ctx.enter_context(nc.psum_tensor("ps_h", [P, CH], F32))
        ps_t = ctx.enter_context(nc.psum_tensor("ps_t", [P, CH], F32))
        ps_x = ctx.enter_context(nc.psum_tensor("ps_x", [P, CH], F32))
        ps_g = ctx.enter_context(nc.psum_tensor("ps_g", [P, CH], F32))

        ids_sb = sb("ids_sb", [P, GROUPS * F], I32)
        idx = sb("idx", [P, F], I32)
        emb = sb("emb", [P, F, D])
        rest = sb("rest", [P, F, D])
        parts = sb("parts", [P, D, X3], BF16)
        xt = sb("xt", [X3, 2 * P * D], BF16)
        choice = sb("choice", [X3, 1 + TILES, X3], BF16)
        id32 = sb("id32", [P, P])
        id16 = sb("id16", [P, P], BF16)
        w_pq = sb("w_pq", [X3, TILES, J])
        w_qp = sb("w_qp", [X3, TILES, J])
        w_pair = sb("w_pair", [X3, TILES, J])
        w_c2 = sb("w_c2", [J, F, K2])
        w_f1 = sb("w_f1", [HX, F, J])
        xa = sb("xa", [X3, 2, COLS])
        z = sb("z", [P, NZ, COLS])
        h_sb = sb("h_sb", [P, CH])
        hx = sb("hx", [P, 2, QUADS, HX])
        xdiag = sb("xdiag", [P, 2, QUADS, QB * F])
        gram = sb("gram", [HX, F, B])
        dense_sb = sb("dense_sb", [P, GROUPS, DENSE])
        w_t1a = sb("w_t1a", [J + DENSE, M1])
        w_t1b = sb("w_t1b", [K2, M1])
        w_t2 = sb("w_t2", [P, M1 // P, M2])
        w_t3 = sb("w_t3", [P, M2 // P])
        bias1 = sb("bias1", [P, M1 // P])
        bias2 = sb("bias2", [P, M2 // P])
        za = sb("za", [J + DENSE, B])
        y_sb = sb("y_sb", [1, B])
        conv2 = sb("conv2", [K2, B])
        top1 = z[:, 0:2, :].rearrange("p a (c b) -> p (a c) b", b=B)
        top2 = z[:, 2, :].rearrange("p (c b) -> p c b", b=B)

        ids_loaded = sem("ids_loaded")
        choice_loaded = sem("choice_loaded")
        ident_loaded = sem("ident_loaded")
        wpair_loaded = sem("wpair_loaded")
        wcin_loaded = sem("wcin_loaded")
        top_loaded = sem("top_loaded")
        out_stored = sem("out_stored")
        idx_ready = sem("idx_ready")
        idx_seen = sem("idx_seen")
        gathered = [sem(f"gathered{p}") for p in range(PIECES)]
        part1_made = sem("part1_made")
        rest_made = sem("rest_made")
        part2_made = sem("part2_made")
        part3_made = sem("part3_made")
        turned = sem("turned")
        turned_copied = sem("turned_copied")
        zero_done = sem("zero_done")
        wqp_zero = sem("wqp_zero")
        wpair_made = sem("wpair_made")
        a_chosen = sem("a_chosen")
        a_copied = sem("a_copied")
        b_chosen = sem("b_chosen")
        z_made = [sem("z_made0"), sem("z_made1")]
        h_summed = sem("h_summed")
        h_copied = sem("h_copied")
        h_turned = sem("h_turned")
        hx_copied = sem("hx_copied")
        x_turned = sem("x_turned")
        x_copied = sem("x_copied")
        gram_done = sem("gram_done")
        gram_copied = sem("gram_copied")
        dense_turned = sem("dense_turned")
        dense_copied = sem("dense_copied")
        cin_done = sem("cin_done")
        cin_copied = sem("cin_copied")
        top1_done = sem("top1_done")
        top1_act = sem("top1_act")
        top1_dve = sem("top1_dve")
        top2_done = sem("top2_done")
        top2_act = sem("top2_act")
        top2_dve = sem("top2_dve")
        y_done = sem("y_done")
        y_copied = sem("y_copied")

        SLOT = [0, 1, 0, 1, 0, 1, 1]
        RANK = [0, 0, 1, 1, 2, 2, 3]
        PER_SLOT = [3, 4]

        def z_count(k, t):
            return k * PER_SLOT[SLOT[t]] + (RANK[t] + 1)

        def xt_base(g):
            return (g % 2) * (P * D)

        block = ctx.enter_context(nc.Block())

        @block.sync
        def _(sp):
            sp.dma_start(ids_sb[:].rearrange("p (g f) -> p g f", g=GROUPS),
                         ids.rearrange("(g p) f -> p g f", p=P)).then_inc(ids_loaded, 16)
            sp.dma_start(choice[:], choices.rearrange("p (m r) -> p m r", r=X3)).then_inc(choice_loaded, 16)
            sp.dma_start(id16[:], ident16).then_inc(ident_loaded, 16)
            sp.dma_start(id32[:], ident).then_inc(ident_loaded, 16)
            for s in range(SHIFTS):
                t, r = s // PER_TILE, s % PER_TILE
                for run_pq, run_qp in pair_rows(s):
                    for dst, (i0, n, row) in ((w_pq, run_pq), (w_qp, run_qp)):
                        if dst is w_qp and s == 0:
                            continue
                        src = w1[row:row + (F + 1) * (n - 1) + 1:F + 1, 0:J]
                        sp.dma_start(dst[F * r + i0:F * r + i0 + n, t, :], src).then_inc(wpair_loaded, 16)
            sp.dma_start(w_c2[:], w2.rearrange("(i j) k -> j i k", j=J)).then_inc(wcin_loaded, 16)
            sp.dma_start(w_f1[J:HX, :, :], w1[:, J:K1].rearrange("(i p) k -> p i k", p=F)).then_inc(wcin_loaded, 16)
            sp.dma_start(dense_sb[:], dense.rearrange("(g p) c -> p g c", p=P)).then_inc(top_loaded, 16)
            sp.dma_start(w_t1a[0:J, :], w_top1[0:J, :]).then_inc(top_loaded, 16)
            sp.dma_start(w_t1a[J:J + DENSE, :], w_top1[J + K2:J + K2 + DENSE, :]).then_inc(top_loaded, 16)
            sp.dma_start(w_t1b[:], w_top1[J:J + K2, :]).then_inc(top_loaded, 16)
            sp.dma_start(w_t2[:], w_top2.rearrange("(c p) m -> p c m", p=P)).then_inc(top_loaded, 16)
            with nc.allow_non_contiguous_dma(reason="a few hundred biases and weights, one per partition"):
                sp.dma_start(w_t3[:], w_top3.rearrange("(c p) o -> p (c o)", p=P)).then_inc(top_loaded, 16)
                sp.dma_start(bias1[:], b_top1.rearrange("(c p) -> p c", p=P)).then_inc(top_loaded, 16)
                sp.dma_start(bias2[:], b_top2.rearrange("(c p) -> p c", p=P)).then_inc(top_loaded, 16)
            sp.wait_ge(y_copied, 1)
            sp.dma_start(out.rearrange("b o -> o b"), y_sb[:]).then_inc(out_stored, 16)
            sp.wait_ge(out_stored, 16)

        TOP_LOADS = 8
        WPAIR_LOADS = sum((1 if s == 0 else 2 * len(pair_rows(s))) for s in range(SHIFTS))

        @block.gpsimd
        def _(gp):
            def gather_group(g, first):
                for p in range(PIECES):
                    if not first:
                        gp.wait_ge(rest_made, PIECES * g + (p + 1 - PIECES))
                    gp.tensor_copy(idx[:, p * FP:(p + 1) * FP],
                                   ids_sb[:, bass.ds(g * F + p * FP, FP)]).then_inc(idx_ready, 1)
                    gp.wait_ge(idx_ready, PIECES * g + (p + 1))
                    gp.sem_inc(idx_seen, 1)
                    for f in range(p * FP, (p + 1) * FP):
                        gp.indirect_dma_start(
                            out=emb[:, f, :], out_offset=None, in_=tables[f],
                            in_offset=bass.IndirectOffsetOnAxis(ap=idx[:, f:f + 1].bitcast(U32), axis=0),
                        ).then_inc(gathered[p], 16)

            gp.wait_ge(ids_loaded, 16)
            gather_group(0, True)
            with gp.Fori(1, GROUPS) as g:
                gather_group(g, False)

        @block.tensor
        def _(pe):
            def turn_batch(g, n):
                bank = (ps_t, ps_x)[n % 2][0:X3, :].bitcast(BF16)
                for e in range(TB):
                    mm = pe.transpose(bank[:, e * P:(e + 1) * P], parts[:, n * TB + e, :], id16[:, :])
                mm.then_inc(turned, 1)

            def choose(k, g, j, which, slot, signal):
                rows = X3 if which == 0 else ROWS[which - 1]
                for c in range(2):
                    mm = pe.matmul(slots[0:rows, slot, c * CH:(c + 1) * CH], choice[:, which, 0:rows],
                                   xt[:, bass.ds(xt_base(g) + (j * COLS + c * CH), CH)], start=True, stop=True)
                mm.then_inc(signal, 1)

            def choose_a(k, g, j):
                choose(k, g, j, 0, 0, a_chosen)

            def choose_b(k, g, j, t, first=False):
                if t == 0:
                    pe.wait_ge(a_copied, k + 1)
                elif t == 1:
                    if not first:
                        pe.wait_ge(z_made[1], PER_SLOT[1] * k)
                else:
                    before = t - 2 if t < 6 else 5
                    pe.wait_ge(z_made[SLOT[t]], z_count(k, before))
                choose(k, g, j, 1 + t, SLOT[t], b_chosen)

            def sum_tile(k, j, t, first):
                if t == 0 and not first:
                    pe.wait_ge(h_copied, k)
                pe.wait_ge(z_made[SLOT[t]], z_count(k, t))
                for c in range(2):
                    mm = pe.matmul(ps_h[c * J:(c + 1) * J, :], w_pair[0:ROWS[t], t, :],
                                   z[0:ROWS[t], (TILES * j + t) % NZ, c * CH:(c + 1) * CH],
                                   start=(t == 0), stop=(t == TILES - 1))
                if t == TILES - 1:
                    mm.then_inc(h_summed, 1)

            def turn_h(kp):
                pe.wait_ge(h_copied, kp + 1)
                pe.wait_ge(hx_copied, kp + 1)
                for q in range(CH // P):
                    mm = pe.transpose(ps_t[:, q * P:(q + 1) * P], h_sb[:, q * P:(q + 1) * P], id32[:, :])
                mm.then_inc(h_turned, 1)

            def turn_x(k, g, j, first):
                if not first:
                    pe.wait_ge(x_copied, k)
                for q in range(QUADS):
                    mm = pe.matmul(ps_x[:, q * F:(q + 1) * F],
                                   xt[:, bass.ds(xt_base(g) + (j * COLS + q * P), P)],
                                   choice[:, 0, 0:F], start=True, stop=True)
                mm.then_inc(x_turned, 1)

            def gram_round(kp, par, r):
                if r == 0:
                    pe.wait_ge(hx_copied, kp + 2)
                    pe.wait_ge(x_copied, kp + 1)
                pe.wait_ge(gram_copied, len(ROUNDS) * kp + r + 1)
                q0, q1 = ROUNDS[r]
                for q in range(q0, q1):
                    mm = pe.matmul(ps_g[0:HX, (q - q0) * QB * F:(q - q0 + 1) * QB * F], hx[:, par, q, :],
                                   xdiag[:, par, q, :], start=True, stop=True)
                mm.then_inc(gram_done, 1)

            def chunk_pair(g, j, first=False, last=False):
                k = g * PAIRS + j
                turns = j == PAIRS - 1 and not last
                gn, jn = (g + 1, 0) if j == PAIRS - 1 else (g, j + 1)
                for t in range(TILES):
                    sum_tile(k, j, t, first)
                    if t + 2 < TILES - 1:
                        choose_b(k, g, j, t + 2)
                    if t == 4 and not last:
                        if turns:
                            pe.wait_ge(turned_copied, (D // TB) * (g + 2))
                        pe.wait_ge(z_made[0], z_count(k, 4))
                        choose_a(k + 1, gn, jn)
                    if t == 5:
                        choose_b(k, g, j, 6)
                    if t == 6 and not last:
                        choose_b(k + 1, gn, jn, 0)
                        choose_b(k + 1, gn, jn, 1)
                    if t == 0 and not first:
                        turn_h(k - 1)
                    if t == 1:
                        turn_x(k, g, j, first)
                    if turns and t == 2:
                        pe.wait_ge(part3_made, PIECES * (g + 2))
                        if not first:
                            pe.wait_ge(hx_copied, k + 1)
                        turn_batch(g + 1, 0)
                        pe.wait_ge(x_copied, k + 1)
                        turn_batch(g + 1, 1)
                    if turns and t == 3:
                        for n in range(2, D // TB):
                            pe.wait_ge(turned_copied, (D // TB) * (g + 1) + (n - 1))
                            turn_batch(g + 1, n)
                    if 3 <= t < 3 + len(ROUNDS) and not first:
                        gram_round(k - 1, (j - 1) % 2, t - 3)

            pe.wait_ge(ident_loaded, 32)
            pe.wait_ge(top_loaded, 16 * TOP_LOADS)
            for g in range(GROUPS):
                mm = pe.transpose(ps_h[0:DENSE, g * P:(g + 1) * P], dense_sb[:, g, :], id32[:, :])
            mm.then_inc(dense_turned, 1)
            pe.wait_ge(part3_made, PIECES)
            for n in range(D // TB):
                if n >= 2:
                    pe.wait_ge(turned_copied, n - 1)
                turn_batch(0, n)
            pe.wait_ge(choice_loaded, 16)
            pe.wait_ge(turned_copied, D // TB)
            choose_a(0, 0, 0)
            choose_b(0, 0, 0, 0)
            choose_b(0, 0, 0, 1, first=True)
            pe.wait_ge(wpair_made, 1)
            pe.wait_ge(dense_copied, 1)
            chunk_pair(0, 0, first=True)
            with pe.Fori(0, GROUPS - 1) as g:
                for j in range(1, PAIRS):
                    chunk_pair(g, j)
                chunk_pair(g + 1, 0)
            for j in range(1, PAIRS):
                chunk_pair(GROUPS - 1, j, last=(j == PAIRS - 1))
            kl = GROUPS * PAIRS - 1
            turn_h(kl)
            for r in range(len(ROUNDS)):
                gram_round(kl, kl % 2, r)

            pe.wait_ge(gram_copied, len(ROUNDS) * (kl + 1) + 1)
            pe.wait_ge(wcin_loaded, 32)
            for i in range(F):
                pe.matmul(slots[:, 0, 0:B], w_c2[:, i, :], gram[0:J, i, :], start=(i == 0), stop=(i == F - 1))
                mm = pe.matmul(slots[0:J, 0, B:2 * B], w_f1[J:HX, i, :], gram[J:HX, i, :],
                               start=(i == 0), stop=(i == F - 1))
            mm.then_inc(cin_done, 1)
            pe.wait_ge(cin_copied, 2)
            top1_banks = [slots[:, 1, 0:B], slots[:, 1, B:2 * B], ps_h[:, :], ps_t[:, :]]
            for m in range(M1 // P):
                pe.matmul(top1_banks[m], w_t1a[:, m * P:(m + 1) * P], za[:, :], start=True, stop=False)
                pe.matmul(top1_banks[m], w_t1b[:, m * P:(m + 1) * P], conv2[:, :],
                          start=False, stop=True).then_inc(top1_done, 1)
            top2_banks = [ps_x[:, :], ps_g[:, :]]
            for c in range(M1 // P):
                if c % 2 == 0:
                    pe.wait_ge(top1_act, c // 2 + 1)
                else:
                    pe.wait_ge(top1_dve, c // 2 + 1)
                for m in range(M2 // P):
                    mm = pe.matmul(top2_banks[m], w_t2[:, c, m * P:(m + 1) * P], top1[:, c, :],
                                   start=(c == 0), stop=(c == M1 // P - 1))
                    if c == M1 // P - 1:
                        mm.then_inc(top2_done, 1)
            pe.wait_ge(top2_act, 1)
            pe.matmul(slots[0:1, 0, 0:B], w_t3[:, 0:1], top2[:, 0, :], start=True, stop=False)
            pe.wait_ge(top2_dve, 1)
            pe.matmul(slots[0:1, 0, 0:B], w_t3[:, 1:2], top2[:, 1, :], start=False, stop=True).then_inc(y_done, 1)

        @block.scalar
        def _(act):
            def part1(g, p):
                act.wait_ge(gathered[p], 16 * FP * (g + 1))
                fs = slice(p * FP, (p + 1) * FP)
                act.copy(parts[:, :, p * FP:(p + 1) * FP].rearrange("p d f -> p f d"),
                         emb[:, fs, :]).then_inc(part1_made, 1)

            def part2(g, p):
                act.wait_ge(rest_made, PIECES * g + (p + 1))
                act.copy(parts[:, :, F + p * FP:F + (p + 1) * FP].rearrange("p d f -> p f d"),
                         rest[:, p * FP:(p + 1) * FP, :]).then_inc(part2_made, 1)

            def copy_turned(g, n):
                act.wait_ge(turned, (D // TB) * g + (n + 1))
                bank = (ps_t, ps_x)[n % 2][0:X3, :].bitcast(BF16)
                dst = xt[:, bass.ds(xt_base(g), P * D)].rearrange("p (b d) -> p d b", d=D)
                act.copy(dst[:, n * TB:(n + 1) * TB, :],
                         bank.rearrange("p (e b) -> p e b", e=TB)).then_inc(turned_copied, 1)

            def copy_a(k, j):
                act.wait_ge(a_chosen, k + 1)
                act.copy(xa[:, j % 2, :], slots[0:X3, 0, :]).then_inc(a_copied, 1)

            def copy_h(kp):
                act.wait_ge(h_summed, kp + 1)
                act.copy(h_sb[:, :], ps_h[:, :]).then_inc(h_copied, 1)

            def copy_hx(kp, par):
                act.wait_ge(h_turned, kp + 1)
                act.copy(hx[:, par, :, 0:J].rearrange("p (c q) m -> p q c m", c=2),
                         ps_t[:, :].rearrange("p (q c m) -> p q c m", c=2, m=J)).then_inc(hx_copied, 1)

            def copy_x(k, par):
                act.wait_ge(x_turned, k + 1)
                src = ps_x[:, 0:QUADS * F].rearrange("p (q f) -> p q f", f=F)
                act.copy(hx[:, par, :, J:HX], src)
                for y in range(QB):
                    rows = slice(y * D, (y + 1) * D)
                    op = act.copy(xdiag[rows, par, :, y * F:(y + 1) * F], src[rows])
                op.then_inc(x_copied, 1)

            def copy_gram(gp_, jp, r):
                kp = gp_ * PAIRS + jp
                act.wait_ge(gram_done, len(ROUNDS) * kp + (r + 1))
                q0, q1 = ROUNDS[r]
                n = (q1 - q0) * QB
                b0 = gp_ * P + (jp * (P // PAIRS) + q0 * QB)
                act.copy(gram[:, :, bass.ds(b0, n)].rearrange("p i b -> p b i"),
                         ps_g[0:HX, 0:n * F].rearrange("p (b i) -> p b i", i=F)).then_inc(gram_copied, 1)

            def chunk_pair(g, j, first=False, last=False):
                k = g * PAIRS + j
                gp_, jp = (g, j - 1) if j else (g - 1, PAIRS - 1)
                splits = j >= 1 and not (isinstance(g, int) and g == GROUPS - 1)
                if not first:
                    copy_h(k - 1)
                    copy_hx(k - 1, jp % 2)
                if splits:
                    part1(g + 1, j - 1)
                copy_x(k, j % 2)
                if splits:
                    part2(g + 1, j - 1)
                if splits and j == PAIRS - 1:
                    for n in range(D // TB):
                        copy_turned(g + 1, n)
                if not first:
                    copy_gram(gp_, jp, 0)
                if not last:
                    copy_a(k + 1, j + 1)
                if not first:
                    copy_gram(gp_, jp, 1)
                    copy_gram(gp_, jp, 2)

            act.sem_inc(hx_copied, 1)
            act.sem_inc(gram_copied, 1)
            act.wait_ge(top_loaded, 16 * TOP_LOADS)
            act.wait_ge(dense_turned, 1)
            act.copy(za[J:J + DENSE, :], ps_h[0:DENSE, :]).then_inc(dense_copied, 1)
            for p in range(PIECES):
                part1(0, p)
                part2(0, p)
            for n in range(D // TB):
                copy_turned(0, n)
            copy_a(0, 0)
            act.wait_ge(zero_done, 1)
            chunk_pair(0, 0, first=True)
            with act.Fori(0, GROUPS - 1) as g:
                for j in range(1, PAIRS):
                    chunk_pair(g, j)
                chunk_pair(g + 1, 0)
            for j in range(1, PAIRS):
                chunk_pair(GROUPS - 1, j, last=(j == PAIRS - 1))
            kl = GROUPS * PAIRS - 1
            copy_h(kl)
            copy_hx(kl, kl % 2)
            for r in range(len(ROUNDS)):
                copy_gram(GROUPS - 1, PAIRS - 1, r)

            act.wait_ge(cin_done, 1)
            act.copy(conv2[:, :], slots[:, 0, 0:B]).then_inc(cin_copied, 1)
            top1_banks = [slots[:, 1, 0:B], slots[:, 1, B:2 * B], ps_h[:, :], ps_t[:, :]]
            for m in range(0, M1 // P, 2):
                act.wait_ge(top1_done, m + 1)
                act.activation(top1[:, m, :], top1_banks[m], ACT.Relu, bias=bias1[:, m:m + 1]).then_inc(top1_act, 1)
            act.wait_ge(top2_done, 1)
            act.activation(top2[:, 0, :], ps_x[:, :], ACT.Relu, bias=bias2[:, 0:1]).then_inc(top2_act, 1)

        @block.vector
        def _(dv):
            def make_rest(g, p):
                dv.wait_ge(part1_made, PIECES * g + (p + 1))
                fs = slice(p * FP, (p + 1) * FP)
                dv.tensor_tensor(rest[:, fs, :], emb[:, fs, :],
                                 parts[:, :, p * FP:(p + 1) * FP].rearrange("p d f -> p f d"),
                                 ALU.subtract).then_inc(rest_made, 1)

            def part3(g, p):
                dv.wait_ge(part2_made, PIECES * g + (p + 1))
                dv.tensor_tensor(parts[:, :, 2 * F + p * FP:2 * F + (p + 1) * FP].rearrange("p d f -> p f d"),
                                 rest[:, p * FP:(p + 1) * FP, :],
                                 parts[:, :, F + p * FP:F + (p + 1) * FP].rearrange("p d f -> p f d"),
                                 ALU.subtract).then_inc(part3_made, 1)

            def make_z(k, j, t):
                if t == 0:
                    dv.wait_ge(a_copied, k + 1)
                dv.wait_ge(b_chosen, TILES * k + (t + 1))
                n = ROWS[t]
                dv.tensor_tensor(z[0:n, (TILES * j + t) % NZ, :], xa[0:n, j % 2, :], slots[0:n, SLOT[t], :],
                                 ALU.mult).then_inc(z_made[SLOT[t]], 1)

            def chunk_pair(g, j):
                k = g * PAIRS + j
                splits = j >= 1 and not (isinstance(g, int) and g == GROUPS - 1)
                for t in range(TILES):
                    make_z(k, j, t)
                    if splits and t == 1:
                        make_rest(g + 1, j - 1)
                    if splits and t == 2:
                        part3(g + 1, j - 1)

            dv.memset(w_qp[0:F, 0, :], 0.0)
            dv.memset(xdiag[:, :, :, :], 0.0).then_inc(zero_done, 1)
            for p in range(PIECES):
                make_rest(0, p)
                part3(0, p)
            dv.wait_ge(wpair_loaded, 16 * WPAIR_LOADS)
            dv.tensor_tensor(w_pair[:, 0:TILES - 1, :], w_pq[:, 0:TILES - 1, :], w_qp[:, 0:TILES - 1, :], ALU.add)
            dv.tensor_tensor(w_pair[0:ROWS[-1], TILES - 1, :], w_pq[0:ROWS[-1], TILES - 1, :],
                             w_qp[0:ROWS[-1], TILES - 1, :], ALU.add).then_inc(wpair_made, 1)
            chunk_pair(0, 0)
            with dv.Fori(0, GROUPS - 1) as g:
                for j in range(1, PAIRS):
                    chunk_pair(g, j)
                chunk_pair(g + 1, 0)
            for j in range(1, PAIRS):
                chunk_pair(GROUPS - 1, j)

            dv.wait_ge(cin_done, 1)
            dv.tensor_copy(za[0:J, :], slots[0:J, 0, B:2 * B]).then_inc(cin_copied, 1)
            top1_banks = [slots[:, 1, 0:B], slots[:, 1, B:2 * B], ps_h[:, :], ps_t[:, :]]
            for m in range(1, M1 // P, 2):
                dv.wait_ge(top1_done, m + 1)
                dv.tensor_scalar(top1[:, m, :], top1_banks[m], bias1[:, m:m + 1], 0.0, ALU.add,
                                 ALU.max).then_inc(top1_dve, 1)
            dv.wait_ge(top2_done, 2)
            dv.tensor_scalar(top2[:, 1, :], ps_g[:, :], bias2[:, 1:2], 0.0, ALU.add, ALU.max).then_inc(top2_dve, 1)
            dv.wait_ge(y_done, 1)
            dv.tensor_copy(y_sb[:, :], slots[0:1, 0, 0:B]).then_inc(y_copied, 1)


TABLES = [f"tbl_{f}" for f in range(F)]
OTHERS = ["dense_ctx", "ids", "W_top1", "b_top1", "W_top2", "b_top2", "W_top3", "L0_rec_W1", "L0_rec_W2"]


def kernel(**inputs):
    import ml_dtypes
    import concourse.bacc as bacc
    from concourse.bass_utils import run_bass_kernel_spmd

    nc = bacc.Bacc("TRN2", target_bir_lowering=False, num_devices=1)
    arrays, ap = {}, {}

    def give(name, a):
        arrays[name] = a
        ap[name] = nc.dram_tensor(name, a.shape, mybir.dt.from_np(a.dtype), kind="ExternalInput").ap()

    for name in TABLES + OTHERS:
        give(name, np.ascontiguousarray(inputs[name]))
    give("choices", field_choices().astype(ml_dtypes.bfloat16))
    give("ident", np.eye(P, dtype=np.float32))
    give("ident16", np.eye(P, dtype=np.float32).astype(ml_dtypes.bfloat16))
    out = nc.dram_tensor("y", (B, 1), F32, kind="ExternalOutput").ap()
    dlrm_tower(nc, ap["dense_ctx"], ap["ids"], [ap[t] for t in TABLES], ap["W_top1"], ap["b_top1"], ap["W_top2"],
               ap["b_top2"], ap["W_top3"], ap["L0_rec_W1"], ap["L0_rec_W2"], ap["choices"], ap["ident"],
               ap["ident16"], out)
    r = run_bass_kernel_spmd(nc, [arrays], core_ids=[0])
    return r.results[0]["y"]
```

```python
from contextlib import ExitStack

import numpy as np
import concourse.bass as bass
from concourse import mybir

F32 = mybir.dt.float32
BF16 = mybir.dt.bfloat16
I32 = mybir.dt.int32
U32 = mybir.dt.uint32
ALU = mybir.AluOpType
ACT = mybir.ActivationFunctionType

P = 128
B = 512
F = 39
D = 32
K1 = 128
J = K1 // 2
K2 = 128
DENSE = 16
GROUPS = B // P
F2 = (F + 1) // 2
PAIRS = 4
COLS = P * D // PAIRS
CH = COLS // 2
QUADS = COLS // P
QB = P // D
SHIFTS = F // 2 + 1
PER_TILE = P // F
TILES = -(-SHIFTS // PER_TILE)
BY_PE = 4
BY_DMA = TILES - BY_PE
ROWS = [F * min(PER_TILE, SHIFTS - PER_TILE * t) for t in range(TILES)]
X3 = 3 * F
CUTS = [0, 17, 32, F]
PIECES = len(CUTS) - 1
M1, M2 = 512, 256
HX = J + F
NZ = 4
ROUNDS = [(0, 3), (3, 6), (6, 8)]
TB = 8

BATCHES = D // TB


def field_choices():
    m = np.zeros((3, F, 1 + TILES, PER_TILE, F), np.float32)
    for i in range(F):
        for r in range(PER_TILE):
            m[:, i, 0, r, i] = 1
            for t in range(TILES):
                if PER_TILE * t + r < SHIFTS:
                    m[:, (i + PER_TILE * t + r) % F, 1 + t, r, i] = 1
    return m.reshape(X3, (1 + TILES) * X3)


def pair_rows(s):
    n = F - s
    runs = [((0, n, s), (0, n, F * s))]
    if s:
        runs.append(((n, s, (F + 1) * n + s - F), (n, s, (F + 1) * n + F * (s - F))))
    return runs


def dlrm_tower(nc, dense, ids, tables, w_top1, b_top1, w_top2, b_top2, w_top3, w1, w2,
               choices, ident, out):
    with ExitStack() as ctx:
        def sb(name, shape, dt=F32):
            return ctx.enter_context(nc.sbuf_tensor(name, shape, dt))

        def sem(name):
            return ctx.enter_context(nc.semaphore(name))

        slots = ctx.enter_context(nc.psum_tensor("slots", [P, 2, COLS], F32))
        ps_h = ctx.enter_context(nc.psum_tensor("ps_h", [P, CH], F32))
        ps_t = ctx.enter_context(nc.psum_tensor("ps_t", [P, CH], F32))
        ps_x = ctx.enter_context(nc.psum_tensor("ps_x", [P, CH], F32))
        ps_g = ctx.enter_context(nc.psum_tensor("ps_g", [P, CH], F32))

        ids_sb = sb("ids_sb", [P, GROUPS * F], I32)
        idx = sb("idx", [P, F], I32)
        emb = sb("emb", [P, F, D])
        rest = sb("rest", [P, F, D])
        parts = sb("parts", [P, D, X3], BF16)
        xt = sb("xt", [X3, 2 * P * D], BF16)
        choice = sb("choice", [X3, 1 + TILES, X3], BF16)
        id32 = sb("id32", [P, P])
        id16 = sb("id16", [P, P], BF16)
        w_pair = sb("w_pair", [X3, TILES, J])
        w_c2 = sb("w_c2", [2 * J, F2, K2])
        w_f1 = sb("w_f1", [HX, F2, J])
        xa = sb("xa", [X3, 2, COLS])
        xb = sb("xb", [X3, 2, BY_DMA, COLS])
        w_pq = xb[:, 0, 0, 0:TILES * J].rearrange("p (t j) -> p t j", j=J)
        w_qp = xb[:, 0, 1, 0:TILES * J].rearrange("p (t j) -> p t j", j=J)
        z = sb("z", [P, NZ, COLS])
        h_sb = sb("h_sb", [P, CH])
        hx = sb("hx", [P, 2, QUADS, HX])
        xdiag = sb("xdiag", [P, 2, QUADS, QB * F])
        gram_g = sb("gram_g", [2 * J, F2, B])
        gram_x = sb("gram_x", [HX, F2, B])
        dense_sb = sb("dense_sb", [P, GROUPS, DENSE])
        w_t1a = sb("w_t1a", [J + DENSE, M1])
        w_t1b = sb("w_t1b", [K2, M1])
        w_t2 = sb("w_t2", [P, M1 // P, M2])
        w_t3 = sb("w_t3", [P, M2 // P])
        bias1 = sb("bias1", [P, M1 // P])
        bias2 = sb("bias2", [P, M2 // P])
        conv2 = z[:, 3, 0:B]
        f1_odd = z[0:J, 3, B:2 * B]
        za = xa[0:J + DENSE, 0, 0:B]
        y_sb = xa[0:1, 1, 0:B]
        top1 = z[:, 0:2, :].rearrange("p a (c b) -> p (a c) b", b=B)
        top2 = z[:, 2, :].rearrange("p (c b) -> p c b", b=B)

        ids_loaded = sem("ids_loaded")
        choice_loaded = sem("choice_loaded")
        id16_made = sem("id16_made")
        ident_loaded = sem("ident_loaded")
        wpair_loaded = sem("wpair_loaded")
        wcin_loaded = sem("wcin_loaded")
        top_loaded = sem("top_loaded")
        out_stored = sem("out_stored")
        idx_ready = sem("idx_ready")
        idx_seen = sem("idx_seen")
        gathered = [sem(f"gathered{p}") for p in range(PIECES)]
        part1_made = sem("part1_made")
        rest_made = sem("rest_made")
        part2_made = sem("part2_made")
        part3_made = sem("part3_made")
        turned = sem("turned")
        turned_copied = sem("turned_copied")
        zero_done = sem("zero_done")
        cin_zeros = sem("cin_zeros")
        wpair_made = sem("wpair_made")
        a_chosen = sem("a_chosen")
        a_copied = sem("a_copied")
        b_chosen = sem("b_chosen")
        z_made = [sem(f"z_made{t}") for t in range(TILES)]
        shifted = [[sem(f"shifted{par}_{t}") for t in range(BY_DMA)] for par in range(2)]
        summed = sem("summed")
        h_copied = sem("h_copied")
        h_turned = sem("h_turned")
        hx_copied = sem("hx_copied")
        x_turned = sem("x_turned")
        x_copied = sem("x_copied")
        gram_done = sem("gram_done")
        g_copied = sem("g_copied")
        x_rows_copied = sem("x_rows_copied")
        dense_turned = sem("dense_turned")
        dense_copied = sem("dense_copied")
        final1_done = sem("final1_done")
        final1_half = sem("final1_half")
        final1_added = sem("final1_added")
        conv2_done = sem("conv2_done")
        conv2_copied = sem("conv2_copied")
        top1_done = sem("top1_done")
        top1_act = sem("top1_act")
        top1_dve = sem("top1_dve")
        top2_done = sem("top2_done")
        top2_act = sem("top2_act")
        top2_dve = sem("top2_dve")
        y_done = sem("y_done")
        y_copied = sem("y_copied")

        def slot_of(j, n):
            return (j * (BY_PE + 1) + n) % 2

        assert PAIRS * (BY_PE + 1) % 2 == 0

        def xt_base(g):
            return (g % 2) * (P * D)

        FIRST_BANKS = [ps_t, ps_x, ps_h, ps_g]

        block = ctx.enter_context(nc.Block())

        def gram_rows(dst, row, odd, g, j, r):
            q0, q1 = ROUNDS[r]
            n, rows, fields = (q1 - q0) * QB, (F if row else J), (F + 1 - odd) // 2
            cols = bass.ds(g * P + (j * (P // PAIRS) + q0 * QB), n)
            return (dst[J * odd:J * odd + rows, 0:fields, cols].rearrange("p i b -> p b i"),
                    ps_g[row:row + rows, 0:n * F].rearrange("p (b i) -> p b i", i=F)[:, :, odd:F:2])

        @block.sync
        def _(sp):
            sp.dma_start(ids_sb[:].rearrange("p (g f) -> p g f", g=GROUPS),
                         ids.rearrange("(g p) f -> p g f", p=P)).then_inc(ids_loaded, 16)
            sp.dma_start(choice[:], choices.rearrange("p (m r) -> p m r", r=X3)).then_inc(choice_loaded, 16)
            sp.dma_start(id32[:], ident).then_inc(ident_loaded, 16)
            for s in range(SHIFTS):
                t, r = s // PER_TILE, s % PER_TILE
                for run_pq, run_qp in pair_rows(s):
                    for dst, (i0, n, row) in ((w_pq, run_pq), (w_qp, run_qp)):
                        if dst is w_qp and s == 0:
                            continue
                        src = w1[row:row + (F + 1) * (n - 1) + 1:F + 1, 0:J]
                        sp.dma_start(dst[F * r + i0:F * r + i0 + n, t, :], src).then_inc(wpair_loaded, 16)
            sp.wait_ge(cin_zeros, 1)
            w2_rows = w2.rearrange("(i j) k -> j i k", j=J)
            w1_rows = w1[:, J:K1].rearrange("(i p) k -> p i k", p=F)
            for odd in range(2):
                n = (F + 1 - odd) // 2
                sp.dma_start(w_c2[J * odd:J * (odd + 1), 0:n, :], w2_rows[:, odd:F:2, :]).then_inc(wcin_loaded, 16)
                sp.dma_start(w_f1[J * odd:J * odd + F, 0:n, :], w1_rows[:, odd:F:2, :]).then_inc(wcin_loaded, 16)
            sp.dma_start(dense_sb[:], dense.rearrange("(g p) c -> p g c", p=P)).then_inc(top_loaded, 16)
            sp.dma_start(w_t1a[0:J, :], w_top1[0:J, :]).then_inc(top_loaded, 16)
            sp.dma_start(w_t1a[J:J + DENSE, :], w_top1[J + K2:J + K2 + DENSE, :]).then_inc(top_loaded, 16)
            sp.dma_start(w_t1b[:], w_top1[J:J + K2, :]).then_inc(top_loaded, 16)
            sp.dma_start(w_t2[:], w_top2.rearrange("(c p) m -> p c m", p=P)).then_inc(top_loaded, 16)
            with nc.allow_non_contiguous_dma(reason="a few hundred biases and weights, one per partition"):
                sp.dma_start(w_t3[:], w_top3.rearrange("(c p) o -> p (c o)", p=P)).then_inc(top_loaded, 16)
                sp.dma_start(bias1[:], b_top1.rearrange("(c p) -> p c", p=P)).then_inc(top_loaded, 16)
                sp.dma_start(bias2[:], b_top2.rearrange("(c p) -> p c", p=P)).then_inc(top_loaded, 16)
            sp.wait_ge(wpair_made, 1)
            def shift_pair(g, j):
                k = g * PAIRS + j
                sp.wait_ge(a_copied, k + 1)
                for t in range(BY_PE, TILES):
                    for r in range(ROWS[t] // F):
                        s = PER_TILE * t + r
                        sp.dma_start(xb[F * r:F * (r + 1), j % 2, t - BY_PE, :],
                                     xa[s:s + F, j % 2, :]).then_inc(shifted[j % 2][t - BY_PE], 16)

            with sp.Fori(0, GROUPS) as g:
                for j in range(PAIRS):
                    shift_pair(g, j)
            sp.wait_ge(y_copied, 1)
            sp.dma_start(out.rearrange("b o -> o b"), y_sb[:]).then_inc(out_stored, 16)
            sp.wait_ge(out_stored, 16)

        TOP_LOADS = 8
        WPAIR_LOADS = sum((1 if s == 0 else 2 * len(pair_rows(s))) for s in range(SHIFTS))

        @block.gpsimd
        def _(gp):
            def gather_group(g, first):
                for p in range(PIECES):
                    if not first:
                        gp.wait_ge(rest_made, PIECES * g + (p + 1 - PIECES))
                    f0, f1 = CUTS[p], CUTS[p + 1]
                    gp.tensor_copy(idx[:, f0:f1], ids_sb[:, bass.ds(g * F + f0, f1 - f0)]).then_inc(idx_ready, 1)
                    gp.wait_ge(idx_ready, PIECES * g + (p + 1))
                    gp.sem_inc(idx_seen, 1)
                    for f in range(f0, f1):
                        gp.indirect_dma_start(
                            out=emb[:, f, :], out_offset=None, in_=tables[f],
                            in_offset=bass.IndirectOffsetOnAxis(ap=idx[:, f:f + 1].bitcast(U32), axis=0),
                        ).then_inc(gathered[p], 16)

            gp.wait_ge(ids_loaded, 16)
            gather_group(0, True)
            with gp.Fori(1, GROUPS) as g:
                gather_group(g, False)

        @block.tensor
        def _(pe):
            def turn_batch(n, where):
                bank = where[0:X3, :].bitcast(BF16)
                for e in range(TB):
                    mm = pe.transpose(bank[:, e * P:(e + 1) * P], parts[:, n * TB + e, :], id16[:, :])
                mm.then_inc(turned, 1)

            def choose(g, j, which, slot, signal):
                rows = X3 if which == 0 else ROWS[which - 1]
                for c in range(2):
                    mm = pe.matmul(slots[0:rows, slot, c * CH:(c + 1) * CH], choice[:, which, 0:rows],
                                   xt[:, bass.ds(xt_base(g) + (j * COLS + c * CH), CH)], start=True, stop=True)
                mm.then_inc(signal, 1)

            def sum_tile(k, j, t, first):
                if t == 0 and not first:
                    pe.wait_ge(h_copied, k)
                for c in range(2):
                    mm = pe.matmul(ps_h[c * J:(c + 1) * J, :], w_pair[0:ROWS[t], t, :],
                                   z[0:ROWS[t], (TILES * j + t) % NZ, c * CH:(c + 1) * CH],
                                   start=(t == 0), stop=(t == TILES - 1))
                mm.then_inc(summed, 1)

            def turn_h(kp):
                pe.wait_ge(h_copied, kp + 1)
                pe.wait_ge(hx_copied, kp + 1)
                for q in range(CH // P):
                    mm = pe.transpose(ps_t[:, q * P:(q + 1) * P], h_sb[:, q * P:(q + 1) * P], id32[:, :])
                mm.then_inc(h_turned, 1)

            def turn_x(g, j):
                for q in range(QUADS):
                    mm = pe.matmul(ps_x[:, q * F:(q + 1) * F],
                                   xt[:, bass.ds(xt_base(g) + (j * COLS + q * P), P)],
                                   choice[:, 0, 0:F], start=True, stop=True)
                mm.then_inc(x_turned, 1)

            def gram_round(kp, par, r):
                if r == 0:
                    pe.wait_ge(hx_copied, kp + 2)
                    pe.wait_ge(x_copied, kp + 1)
                pe.wait_ge(g_copied, len(ROUNDS) * kp + r + 1)
                pe.wait_ge(x_rows_copied, len(ROUNDS) * kp + r + 1)
                q0, q1 = ROUNDS[r]
                for q in range(q0, q1):
                    mm = pe.matmul(ps_g[0:HX, (q - q0) * QB * F:(q - q0 + 1) * QB * F], hx[:, par, q, :],
                                   xdiag[:, par, q, :], start=True, stop=True)
                mm.then_inc(gram_done, 1)

            def chunk_pair(g, j, first=False, last=False):
                k = g * PAIRS + j
                turns = j == PAIRS - 1 and not last
                gn, jn = (g + 1, 0) if j == PAIRS - 1 else (g, j + 1)
                for t in range(TILES):
                    pe.wait_ge(z_made[t], k + 1)
                    if t + 2 < BY_PE:
                        choose(g, j, t + 3, slot_of(j, t + 2), b_chosen)
                    if t == (4 if j == PAIRS - 1 else 2) and not last:
                        if turns:
                            pe.wait_ge(turned_copied, BATCHES * (g + 2))
                        choose(gn, jn, 0, slot_of(j, BY_PE), a_chosen)
                    if t == 5 and not last:
                        choose(gn, jn, 1, slot_of(j + 1, 0), b_chosen)
                    sum_tile(k, j, t, first)
                    if t == 0 and not first:
                        turn_h(k - 1)
                    if t == 6 and not last:
                        pe.wait_ge(a_copied, k + 2)
                        choose(gn, jn, 2, slot_of(j + 1, 1), b_chosen)
                        pe.wait_ge(x_copied, k + 1)
                        turn_x(gn, jn)
                    if turns and t == 1:
                        pe.wait_ge(part3_made, PIECES * (g + 2))
                        pe.wait_ge(hx_copied, k + 1)
                        turn_batch(0, ps_t)
                    if turns and t == 2:
                        pe.wait_ge(x_copied, k + 1)
                        turn_batch(1, ps_x)
                        pe.wait_ge(turned_copied, BATCHES * (g + 1) + 1)
                        turn_batch(2, ps_t)
                    if turns and t == 3:
                        pe.wait_ge(turned_copied, BATCHES * (g + 1) + 2)
                        turn_batch(3, ps_x)
                    if 3 <= t < 3 + len(ROUNDS) and not first:
                        gram_round(k - 1, (j - 1) % 2, t - 3)

            pe.wait_ge(id16_made, 1)
            pe.wait_ge(part3_made, PIECES)
            for n in range(BATCHES):
                turn_batch(n, FIRST_BANKS[n])
            pe.wait_ge(choice_loaded, 16)
            pe.wait_ge(turned_copied, BATCHES)
            choose(0, 0, 0, slot_of(-1, BY_PE), a_chosen)
            choose(0, 0, 1, slot_of(0, 0), b_chosen)
            pe.wait_ge(a_copied, 1)
            choose(0, 0, 2, slot_of(0, 1), b_chosen)
            turn_x(0, 0)
            pe.wait_ge(wpair_made, 1)
            chunk_pair(0, 0, first=True)
            with pe.Fori(0, GROUPS - 1) as g:
                for j in range(1, PAIRS):
                    chunk_pair(g, j)
                chunk_pair(g + 1, 0)
            for j in range(1, PAIRS):
                chunk_pair(GROUPS - 1, j, last=(j == PAIRS - 1))
            kl = GROUPS * PAIRS - 1
            turn_h(kl)
            for r in range(len(ROUNDS)):
                gram_round(kl, kl % 2, r)

            pe.wait_ge(top_loaded, 16 * TOP_LOADS)
            for g in range(GROUPS):
                mm = pe.transpose(ps_h[0:DENSE, g * P:(g + 1) * P], dense_sb[:, g, :], id32[:, :])
            mm.then_inc(dense_turned, 1)

            pe.wait_ge(g_copied, len(ROUNDS) * (kl + 1) + 1)
            pe.wait_ge(x_rows_copied, len(ROUNDS) * (kl + 1) + 1)
            pe.wait_ge(wcin_loaded, 64)
            for i in range(F2):
                half = slice(J * (i % 2), J * (i % 2 + 1))
                mm = pe.matmul(slots[half, 0, B:2 * B], w_f1[:, i, :], gram_x[:, i, :],
                               start=(i < 2), stop=(i >= F2 - 2))
            mm.then_inc(final1_done, 1)
            for i in range(F2):
                mm = pe.matmul(slots[:, 0, 0:B], w_c2[:, i, :], gram_g[:, i, :], start=(i == 0), stop=(i == F2 - 1))
            mm.then_inc(conv2_done, 1)
            pe.wait_ge(dense_copied, 1)
            pe.wait_ge(final1_added, 1)
            top1_banks = [slots[:, 1, 0:B], slots[:, 1, B:2 * B], ps_h[:, :], ps_t[:, :]]
            for m in range(M1 // P):
                pe.matmul(top1_banks[m], w_t1a[:, m * P:(m + 1) * P], za[:, :], start=True, stop=False)
            pe.wait_ge(conv2_copied, 1)
            for m in range(M1 // P):
                pe.matmul(top1_banks[m], w_t1b[:, m * P:(m + 1) * P], conv2[:, :],
                          start=False, stop=True).then_inc(top1_done, 1)
            top2_banks = [ps_x[:, :], ps_g[:, :]]
            for c in range(M1 // P):
                if c % 2 == 0:
                    pe.wait_ge(top1_act, c // 2 + 1)
                else:
                    pe.wait_ge(top1_dve, c // 2 + 1)
                for m in range(M2 // P):
                    mm = pe.matmul(top2_banks[m], w_t2[:, c, m * P:(m + 1) * P], top1[:, c, :],
                                   start=(c == 0), stop=(c == M1 // P - 1))
                    if c == M1 // P - 1:
                        mm.then_inc(top2_done, 1)
            pe.wait_ge(top2_act, 1)
            pe.matmul(slots[0:1, 0, 0:B], w_t3[:, 0:1], top2[:, 0, :], start=True, stop=False)
            pe.wait_ge(top2_dve, 1)
            pe.matmul(slots[0:1, 0, 0:B], w_t3[:, 1:2], top2[:, 1, :], start=False, stop=True).then_inc(y_done, 1)

        @block.scalar
        def _(act):
            def part1(g, p):
                act.wait_ge(gathered[p], 16 * (CUTS[p + 1] - CUTS[p]) * (g + 1))
                fs = slice(CUTS[p], CUTS[p + 1])
                act.copy(parts[:, :, CUTS[p]:CUTS[p + 1]].rearrange("p d f -> p f d"),
                         emb[:, fs, :]).then_inc(part1_made, 1)

            def part2(g, p):
                act.wait_ge(rest_made, PIECES * g + (p + 1))
                act.copy(parts[:, :, F + CUTS[p]:F + CUTS[p + 1]].rearrange("p d f -> p f d"),
                         rest[:, CUTS[p]:CUTS[p + 1], :]).then_inc(part2_made, 1)

            def copy_turned(g, n, where):
                act.wait_ge(turned, BATCHES * g + (n + 1))
                bank = where[0:X3, :].bitcast(BF16)
                dst = xt[:, bass.ds(xt_base(g), P * D)].rearrange("p (b d) -> p d b", d=D)
                act.copy(dst[:, n * TB:(n + 1) * TB, :],
                         bank.rearrange("p (e b) -> p e b", e=TB)).then_inc(turned_copied, 1)

            def copy_a(k, j):
                act.wait_ge(a_chosen, k + 1)
                act.copy(xa[:, j % 2, :], slots[0:X3, slot_of(j - 1, BY_PE), :]).then_inc(a_copied, 1)

            def copy_h(kp):
                act.wait_ge(summed, TILES * (kp + 1))
                act.copy(h_sb[:, :], ps_h[:, :]).then_inc(h_copied, 1)

            def copy_hx(kp, par):
                act.wait_ge(h_turned, kp + 1)
                act.copy(hx[:, par, :, 0:J].rearrange("p (c q) m -> p q c m", c=2),
                         ps_t[:, :].rearrange("p (q c m) -> p q c m", c=2, m=J)).then_inc(hx_copied, 1)

            def copy_x(k, par):
                act.wait_ge(x_turned, k + 1)
                src = ps_x[:, 0:QUADS * F].rearrange("p (q f) -> p q f", f=F)
                act.copy(hx[:, par, :, J:HX], src)
                for y in range(QB):
                    rows = slice(y * D, (y + 1) * D)
                    op = act.copy(xdiag[rows, par, :, y * F:(y + 1) * F], src[rows])
                op.then_inc(x_copied, 1)

            def copy_g(gp_, jp, r):
                kp = gp_ * PAIRS + jp
                act.wait_ge(gram_done, len(ROUNDS) * kp + (r + 1))
                act.copy(*gram_rows(gram_g, 0, 0, gp_, jp, r))
                act.copy(*gram_rows(gram_g, 0, 1, gp_, jp, r)).then_inc(g_copied, 1)
                if r == len(ROUNDS) - 1:
                    act.copy(*gram_rows(gram_x, J, 0, gp_, jp, r))
                    act.copy(*gram_rows(gram_x, J, 1, gp_, jp, r)).then_inc(x_rows_copied, 1)

            def chunk_pair(g, j, first=False, last=False):
                k = g * PAIRS + j
                gp_, jp = (g, j - 1) if j else (g - 1, PAIRS - 1)
                splits = not (isinstance(g, int) and g == GROUPS - 1)
                if not first:
                    copy_h(k - 1)
                copy_x(k, j % 2)
                if not first:
                    copy_hx(k - 1, jp % 2)
                if splits and j == PAIRS - 1:
                    for n in range(BATCHES):
                        copy_turned(g + 1, n, (ps_t, ps_x)[n % 2])
                if splits and j == 1:
                    part1(g + 1, 0)
                if splits and j == 2:
                    part1(g + 1, 1)
                if j < PAIRS - 1:
                    copy_a(k + 1, j + 1)
                if splits and j == 1:
                    part2(g + 1, 0)
                if splits and j == 2:
                    part1(g + 1, 2)
                    part2(g + 1, 1)
                if not first:
                    copy_g(gp_, jp, 0)
                if j == PAIRS - 1 and not last:
                    copy_a(k + 1, j + 1)
                if splits and j == 2:
                    part2(g + 1, 2)
                if not first:
                    copy_g(gp_, jp, 1)
                    copy_g(gp_, jp, 2)

            act.sem_inc(hx_copied, 1)
            act.sem_inc(g_copied, 1)
            act.sem_inc(x_rows_copied, 1)
            act.wait_ge(ident_loaded, 16)
            act.copy(id16[:, :], id32[:, :]).then_inc(id16_made, 1)
            for p in range(PIECES):
                part1(0, p)
                part2(0, p)
            for n in range(0, BATCHES, 2):
                copy_turned(0, n, FIRST_BANKS[n])
            copy_a(0, 0)
            act.wait_ge(zero_done, 1)
            chunk_pair(0, 0, first=True)
            with act.Fori(0, GROUPS - 1) as g:
                for j in range(1, PAIRS):
                    chunk_pair(g, j)
                chunk_pair(g + 1, 0)
            for j in range(1, PAIRS):
                chunk_pair(GROUPS - 1, j, last=(j == PAIRS - 1))
            kl = GROUPS * PAIRS - 1
            copy_h(kl)
            copy_hx(kl, kl % 2)
            for r in range(len(ROUNDS)):
                copy_g(GROUPS - 1, PAIRS - 1, r)

            act.wait_ge(dense_turned, 1)
            act.copy(za[J:J + DENSE, :], ps_h[0:DENSE, :]).then_inc(dense_copied, 1)

            act.wait_ge(final1_done, 1)
            act.copy(f1_odd[:, :], slots[J:2 * J, 0, B:2 * B]).then_inc(final1_half, 1)
            act.wait_ge(conv2_done, 1)
            act.copy(conv2[:, :], slots[:, 0, 0:B]).then_inc(conv2_copied, 1)
            top1_banks = [slots[:, 1, 0:B], slots[:, 1, B:2 * B], ps_h[:, :], ps_t[:, :]]
            for m in range(0, M1 // P, 2):
                act.wait_ge(top1_done, m + 1)
                act.activation(top1[:, m, :], top1_banks[m], ACT.Relu, bias=bias1[:, m:m + 1]).then_inc(top1_act, 1)
            act.wait_ge(top2_done, 1)
            act.activation(top2[:, 0, :], ps_x[:, :], ACT.Relu, bias=bias2[:, 0:1]).then_inc(top2_act, 1)

        @block.vector
        def _(dv):
            def make_rest(g, p):
                dv.wait_ge(part1_made, PIECES * g + (p + 1))
                fs = slice(CUTS[p], CUTS[p + 1])
                dv.tensor_tensor(rest[:, fs, :], emb[:, fs, :],
                                 parts[:, :, CUTS[p]:CUTS[p + 1]].rearrange("p d f -> p f d"),
                                 ALU.subtract).then_inc(rest_made, 1)

            def part3(g, p):
                dv.wait_ge(part2_made, PIECES * g + (p + 1))
                dv.tensor_tensor(parts[:, :, 2 * F + CUTS[p]:2 * F + CUTS[p + 1]].rearrange("p d f -> p f d"),
                                 rest[:, CUTS[p]:CUTS[p + 1], :],
                                 parts[:, :, F + CUTS[p]:F + CUTS[p + 1]].rearrange("p d f -> p f d"),
                                 ALU.subtract).then_inc(part3_made, 1)

            def make_z(k, g, j, t):
                if t == 0:
                    dv.wait_ge(a_copied, k + 1)
                n = ROWS[t]
                if t >= NZ:
                    dv.wait_ge(summed, TILES * k + (t - NZ + 1))
                if t < BY_PE:
                    dv.wait_ge(b_chosen, BY_PE * k + (t + 1))
                    b_rows = slots[0:n, slot_of(j, t), :]
                else:
                    dv.wait_ge(shifted[j % 2][t - BY_PE], 16 * (n // F) * (PAIRS // 2 * g + (j // 2 + 1)))
                    b_rows = xb[0:n, j % 2, t - BY_PE, :]
                dv.tensor_tensor(z[0:n, (TILES * j + t) % NZ, :], xa[0:n, j % 2, :], b_rows,
                                 ALU.mult).then_inc(z_made[t], 1)

            def copy_turned(n):
                dv.wait_ge(turned, n + 1)
                dst = xt[:, 0:P * D].rearrange("p (b d) -> p d b", d=D)
                dv.tensor_copy(dst[:, n * TB:(n + 1) * TB, :],
                               FIRST_BANKS[n][0:X3, :].bitcast(BF16).rearrange("p (e b) -> p e b", e=TB)
                               ).then_inc(turned_copied, 1)

            def copy_x_rows(g, j, r):
                dv.wait_ge(gram_done, len(ROUNDS) * (g * PAIRS + j) + (r + 1))
                dv.tensor_copy(*gram_rows(gram_x, J, 0, g, j, r))
                dv.tensor_copy(*gram_rows(gram_x, J, 1, g, j, r)).then_inc(x_rows_copied, 1)

            def chunk_pair(g, j, first=False):
                k = g * PAIRS + j
                gp_, jp = (g, j - 1) if j else (g - 1, PAIRS - 1)
                splits = not (isinstance(g, int) and g == GROUPS - 1)
                for t in range(TILES):
                    make_z(k, g, j, t)
                    if t == 5 and not first:
                        copy_x_rows(gp_, jp, 0)
                    if t == 6 and not first:
                        copy_x_rows(gp_, jp, 1)
                    if splits and j == 1:
                        if t == 3:
                            make_rest(g + 1, 0)
                        if t == 5:
                            part3(g + 1, 0)
                    if splits and j == 2:
                        if t == 2:
                            make_rest(g + 1, 1)
                        if t == 4:
                            make_rest(g + 1, 2)
                            part3(g + 1, 1)
                        if t == 6:
                            part3(g + 1, 2)

            dv.memset(w_c2[J:2 * J, F2 - 1, :], 0.0)
            dv.memset(w_f1[:, :, :], 0.0).then_inc(cin_zeros, 1)
            dv.memset(w_qp[0:F, 0, :], 0.0)
            dv.memset(xdiag[:, :, :, :], 0.0).then_inc(zero_done, 1)
            dv.memset(gram_g[J:2 * J, F2 - 1, :], 0.0)
            dv.memset(gram_x[J:HX, F2 - 1, :], 0.0)
            dv.memset(gram_x[32:J, :, :], 0.0)
            for p in range(PIECES):
                make_rest(0, p)
                part3(0, p)
            for n in range(1, BATCHES, 2):
                copy_turned(n)
            dv.wait_ge(wpair_loaded, 16 * WPAIR_LOADS)
            dv.tensor_tensor(w_pair[:, 0:TILES - 1, :], w_pq[:, 0:TILES - 1, :], w_qp[:, 0:TILES - 1, :], ALU.add)
            dv.tensor_tensor(w_pair[0:ROWS[-1], TILES - 1, :], w_pq[0:ROWS[-1], TILES - 1, :],
                             w_qp[0:ROWS[-1], TILES - 1, :], ALU.add).then_inc(wpair_made, 1)
            chunk_pair(0, 0, first=True)
            with dv.Fori(0, GROUPS - 1) as g:
                for j in range(1, PAIRS):
                    chunk_pair(g, j)
                chunk_pair(g + 1, 0)
            for j in range(1, PAIRS):
                chunk_pair(GROUPS - 1, j)

            for r in range(len(ROUNDS) - 1):
                copy_x_rows(GROUPS - 1, PAIRS - 1, r)
            dv.wait_ge(final1_half, 1)
            dv.tensor_tensor(za[0:J, :], slots[0:J, 0, B:2 * B], f1_odd[:, :], ALU.add).then_inc(final1_added, 1)
            top1_banks = [slots[:, 1, 0:B], slots[:, 1, B:2 * B], ps_h[:, :], ps_t[:, :]]
            for m in range(1, M1 // P, 2):
                dv.wait_ge(top1_done, m + 1)
                dv.tensor_scalar(top1[:, m, :], top1_banks[m], bias1[:, m:m + 1], 0.0, ALU.add,
                                 ALU.max).then_inc(top1_dve, 1)
            dv.wait_ge(top2_done, 2)
            dv.tensor_scalar(top2[:, 1, :], ps_g[:, :], bias2[:, 1:2], 0.0, ALU.add, ALU.max).then_inc(top2_dve, 1)
            dv.wait_ge(y_done, 1)
            dv.tensor_copy(y_sb[:, :], slots[0:1, 0, 0:B]).then_inc(y_copied, 1)


TABLES = [f"tbl_{f}" for f in range(F)]
OTHERS = ["dense_ctx", "ids", "W_top1", "b_top1", "W_top2", "b_top2", "W_top3", "L0_rec_W1", "L0_rec_W2"]


def kernel(**inputs):
    import ml_dtypes
    import concourse.bacc as bacc
    from concourse.bass_utils import run_bass_kernel_spmd

    nc = bacc.Bacc("TRN2", target_bir_lowering=False, num_devices=1)
    arrays, ap = {}, {}

    def give(name, a):
        arrays[name] = a
        ap[name] = nc.dram_tensor(name, a.shape, mybir.dt.from_np(a.dtype), kind="ExternalInput").ap()

    for name in TABLES + OTHERS:
        give(name, np.ascontiguousarray(inputs[name]))
    give("choices", field_choices().astype(ml_dtypes.bfloat16))
    give("ident", np.eye(P, dtype=np.float32))
    out = nc.dram_tensor("y", (B, 1), F32, kind="ExternalOutput").ap()
    dlrm_tower(nc, ap["dense_ctx"], ap["ids"], [ap[t] for t in TABLES], ap["W_top1"], ap["b_top1"], ap["W_top2"],
               ap["b_top2"], ap["W_top3"], ap["L0_rec_W1"], ap["L0_rec_W2"], ap["choices"], ap["ident"], out)
    r = run_bass_kernel_spmd(nc, [arrays], core_ids=[0])
    return r.results[0]["y"]
```

```python
from contextlib import ExitStack

import numpy as np
import concourse.bass as bass
from concourse import mybir

F32 = mybir.dt.float32
BF16 = mybir.dt.bfloat16
F16 = mybir.dt.float16
I32 = mybir.dt.int32
U32 = mybir.dt.uint32
ALU = mybir.AluOpType
ACT = mybir.ActivationFunctionType
AXES = mybir.AxisListType

P = 128
B = 512
F = 39
D = 32
K1 = 128
J = K1 // 2
K2 = 128
DENSE = 16
GROUPS = B // P
F2 = (F + 1) // 2
PAIRS = 4
COLS = P * D // PAIRS
CH = COLS // 2
QUADS = COLS // P
QB = P // D
SHIFTS = F // 2 + 1
PER_TILE = P // F
TILES = -(-SHIFTS // PER_TILE)
BY_PE = 3
BY_DMA = TILES - BY_PE
ROWS = [F * min(PER_TILE, SHIFTS - PER_TILE * t) for t in range(TILES)]
X3 = 3 * F
CUTS = [0, 17, 31, F]
PIECES = len(CUTS) - 1
M1, M2 = 512, 256
HX = J + F
NZ = 4
ROUNDS = [(0, 3), (3, 6), (6, 8)]
GRAM_STEPS = [3, 5, 6]
TB = 8

BATCHES = D // TB
WARM_UPS = 10
HOT_ROWS = 125
HOT_MAX = 10
HOT_PRODUCTS = 124
HOT_BANK = 5


def hot_fields(rows):
    chosen = [[] for _ in range(PIECES)]
    products = 0
    for f in sorted(range(F), key=lambda f: (rows[f], -f)):
        p = sum(f >= c for c in CUTS[1:])
        n = rows[f] // HOT_ROWS
        if rows[f] % HOT_ROWS == 0 and n <= HOT_MAX and products + n <= HOT_PRODUCTS and len(chosen[p]) < HOT_BANK:
            chosen[p].append(f)
            products += n
    by_piece = [[(n, sorted(f for f in fs if rows[f] // HOT_ROWS == n))
                 for n in sorted({rows[f] // HOT_ROWS for f in fs})] for fs in chosen]
    return by_piece, [CUTS[p + 1] - CUTS[p] - len(chosen[p]) for p in range(PIECES)]


def runs_of(fields):
    runs = []
    for c, f in enumerate(sorted(fields)):
        if runs and runs[-1][0] + runs[-1][1] == f:
            runs[-1] = (runs[-1][0], runs[-1][1] + 1, runs[-1][2])
        else:
            runs.append((f, 1, c))
    return runs


def field_choices():
    m = np.zeros((3, F, 1 + TILES, PER_TILE, F), np.float32)
    for i in range(F):
        for r in range(PER_TILE):
            m[:, i, 0, r, i] = 1
            for t in range(TILES):
                if PER_TILE * t + r < SHIFTS:
                    m[:, (i + PER_TILE * t + r) % F, 1 + t, r, i] = 1
    return m.reshape(X3, (1 + TILES) * X3)


def by_pairs(w1):
    out = np.zeros((2, PER_TILE, F, TILES, J), w1.dtype)
    w = w1.reshape(F, F, K1)[:, :, 0:J]
    i = np.arange(F)
    for s in range(SHIFTS):
        t, r = s // PER_TILE, s % PER_TILE
        out[0, r, :, t] = w[i, (i + s) % F]
        if s:
            out[1, r, :, t] = w[(i + s) % F, i]
    return out.reshape(2, X3, TILES * J)


def dlrm_tower(nc, dense, ids, tables, w_top1, b_top1, w_top2, b_top2, w_top3, w1, w1_pairs, w2,
               choices, ident, row_numbers, out):
    hot_by_piece, gathers0 = hot_fields([t.shape[0] for t in tables])
    hot = [f for classes in hot_by_piece for _, fs in classes for f in fs]
    hot_counts = sorted({n for classes in hot_by_piece for n, _ in classes})
    with ExitStack() as ctx:
        def sb(name, shape, dt=F32):
            return ctx.enter_context(nc.sbuf_tensor(name, shape, dt))

        def sem(name):
            return ctx.enter_context(nc.semaphore(name))

        slots = ctx.enter_context(nc.psum_tensor("slots", [P, 2, COLS], F32))
        ps_h = ctx.enter_context(nc.psum_tensor("ps_h", [P, CH], F32))
        ps_t = ctx.enter_context(nc.psum_tensor("ps_t", [P, CH], F32))
        ps_x = ctx.enter_context(nc.psum_tensor("ps_x", [P, CH], F32))
        ps_g = ctx.enter_context(nc.psum_tensor("ps_g", [P, CH], F32))

        ids_sb = sb("ids_sb", [P, GROUPS * F], I32)
        idx = sb("idx", [P, F], I32)
        emb = sb("emb", [P, F, D])
        rest = sb("rest", [P, F, D])
        parts = sb("parts", [P, D, X3], BF16)
        xt = sb("xt", [X3, 2 * P * D], BF16)
        late = xt[:, 0:P * D].bitcast(F32)
        w_f1 = late[0:HX, 0:F2 * J].rearrange("p (i k) -> p i k", k=J)
        w_t1a = late[0:J + DENSE, F2 * J:F2 * J + M1]
        choice = sb("choice", [X3, 1 + TILES, X3], BF16)
        id32 = sb("id32", [P, P])
        id16 = sb("id16", [P, P], BF16)
        w_pair = sb("w_pair", [X3, TILES, J])
        w_c2 = sb("w_c2", [2 * J, F2, K2])
        xa = sb("xa", [X3, 2, COLS])
        xb = sb("xb", [X3, 2, BY_DMA, COLS])
        w_pq = xb[:, 0, 0, 0:TILES * J].rearrange("p (t j) -> p t j", j=J)
        w_qp = xb[:, 0, 1, 0:TILES * J].rearrange("p (t j) -> p t j", j=J)
        z = sb("z", [P, NZ, COLS])
        h_sb = sb("h_sb", [P, CH])
        hx = sb("hx", [P, 2, QUADS, P])
        xdiag = sb("xdiag", [P, 2, QUADS, QB * F])
        gram_g = sb("gram_g", [2 * J, F2, B])
        gram_x = sb("gram_x", [P, F2, B])
        dense_sb = sb("dense_sb", [P, GROUPS, DENSE])
        w_t1b = rest[:, :, :].rearrange("p f d -> p (f d)")[:, 0:M1]
        w_t2 = emb[:, :, :].rearrange("p f d -> p (f d)")[:, 0:M1 // P * M2].rearrange("p (c m) -> p c m", m=M2)
        hot_rows = [sum(n * len(fs) for n, fs in classes) for classes in hot_by_piece]
        hot_table, hot_parts, at = [], [], 0
        z_cols = z[0:HOT_ROWS, :, :].rearrange("p a c -> p (a c)")
        gx_cols = gram_x[0:HOT_ROWS, 0:F2 - 1, :].rearrange("p i b -> p (i b)")
        for p in range(PIECES):
            a, b = at * D, (at + hot_rows[p]) * D
            hot_table.append(z_cols[:, a:b].rearrange("p (r d) -> p r d", d=D))
            hot_parts.append(gx_cols.bitcast(BF16)[:, 3 * a:3 * b].rearrange(
                "p (r t d) -> p r t d", t=3, d=D))
            at += hot_rows[p]
        id_cols = gx_cols.bitcast(F16)[:, 3 * at * D:3 * at * D + len(hot) * P]
        ids_f = sb("ids_f", [P, F])
        row_no = sb("row_no", [HOT_ROWS, len(hot_counts), HOT_MAX])

        def hot_row0(p, f):
            at = 0
            for n, fs in hot_by_piece[p]:
                for g in fs:
                    if g == f:
                        return at
                    at += n

        hot_steps = []
        at = 0
        onehots = gram_g[0:HOT_ROWS, 0:F2 - 1, :].rearrange("p i b -> p (i b)").bitcast(BF16)
        for p in range(PIECES):
            for n, fs in hot_by_piece[p]:
                for k in range(n):
                    hot_steps.append((p, n, k, fs, onehots[:, at:at + len(fs) * P].rearrange(
                        "p (f b) -> p f b", b=P)))
                    at += len(fs) * P
        hot_pieces = [p for p in range(PIECES) if hot_by_piece[p]]

        def hot_runs_until(p):
            return sum(len(runs_of([f for _, fs in hot_by_piece[q] for f in fs])) for q in range(p + 1))

        HOT_BANKS = [ps_t, ps_h, ps_g]

        def hot_place(p, f):
            c = sorted(g for _, fs in hot_by_piece[p] for g in fs).index(f)
            return HOT_BANKS[p][:, c * 3 * D:(c + 1) * 3 * D]
        w_t3 = sb("w_t3", [P, M2 // P])
        bias1 = sb("bias1", [P, M1 // P])
        bias2 = sb("bias2", [P, M2 // P])
        conv2 = z[:, 3, 0:B]
        f1_odd = z[0:J, 3, B:2 * B]
        za = xa[0:J + DENSE, 0, 0:B]
        y_sb = xa[0:1, 1, 0:B]
        top1 = z[:, 0:2, :].rearrange("p a (c b) -> p (a c) b", b=B)
        top2 = z[:, 2, :].rearrange("p (c b) -> p c b", b=B)

        ids_loaded = sem("ids_loaded")
        choice_loaded = sem("choice_loaded")
        id16_made = sem("id16_made")
        ident_loaded = sem("ident_loaded")
        wpair_loaded = sem("wpair_loaded")
        wcin_loaded = sem("wcin_loaded")
        top_loaded = sem("top_loaded")
        out_stored = sem("out_stored")
        idx_ready = sem("idx_ready")
        row_no_loaded = sem("row_no_loaded")
        hot_tables_loaded = [sem(f"hot_tables_loaded{p}") for p in range(PIECES)]
        hot_part1_made = sem("hot_part1_made")
        hot_rest_made = sem("hot_rest_made")
        hot_part2_made = sem("hot_part2_made")
        hot_part3_made = sem("hot_part3_made")
        ids_f_made = sem("ids_f_made")
        ids_spread = sem("ids_spread")
        ids_copied = sem("ids_copied")
        looked_up = sem("looked_up")
        hot_made = sem("hot_made")
        hot_summed = [sem(f"hot_summed{p}") for p in range(PIECES)]
        idx_seen = sem("idx_seen")
        gathered = [sem(f"gathered{p}") for p in range(PIECES)]
        part1_made = sem("part1_made")
        rest_made = sem("rest_made")
        part2_made = sem("part2_made")
        part3_made = sem("part3_made")
        turned = sem("turned")
        turned_copied = sem("turned_copied")
        first_copied = sem("first_copied")
        hx_zeros = sem("hx_zeros")
        cin_zeros = sem("cin_zeros")
        late_zeros = sem("late_zeros")
        wpair_made = sem("wpair_made")
        a_chosen = sem("a_chosen")
        a_copied = sem("a_copied")
        b_chosen = sem("b_chosen")
        z_made = [sem(f"z_made{t}") for t in range(TILES)]
        shifted = [[sem(f"shifted{par}_{t}") for t in range(BY_DMA)] for par in range(2)]
        summed = sem("summed")
        h_copied = sem("h_copied")
        h_turned = sem("h_turned")
        hx_copied = sem("hx_copied")
        x_turned = sem("x_turned")
        x_copied = sem("x_copied")
        gram_done = sem("gram_done")
        g_copied = sem("g_copied")
        x_rows_copied = sem("x_rows_copied")
        dense_turned = sem("dense_turned")
        dense_copied = sem("dense_copied")
        final1_done = sem("final1_done")
        final1_half = sem("final1_half")
        final1_added = sem("final1_added")
        conv2_done = sem("conv2_done")
        conv2_copied = sem("conv2_copied")
        top1_done = sem("top1_done")
        top1_act = sem("top1_act")
        top1_dve = sem("top1_dve")
        top2_done = sem("top2_done")
        top2_act = sem("top2_act")
        top2_dve = sem("top2_dve")
        y_done = sem("y_done")
        y_copied = sem("y_copied")

        def slot_of(j, n):
            return (j * (BY_PE + 1) + n) % 2

        assert PAIRS * (BY_PE + 1) % 2 == 0

        def xt_base(g):
            return (g % 2) * (P * D)

        FIRST_BANKS = [ps_t, ps_x, ps_h, ps_g]

        LAST_BANKS = [ps_g, ps_x, slots[:, 1, 0:CH]]
        ps_dense = slots[0:DENSE, 1, CH:2 * CH]

        def first_turned(n, pair0):
            bs = slice(0, P // PAIRS) if pair0 else slice(P // PAIRS, P)
            dst = xt[:, 0:P * D].rearrange("p (b d) -> p d b", d=D)
            bank = FIRST_BANKS[n][0:X3, :].bitcast(BF16).rearrange("p (e b) -> p e b", e=TB)
            return dst[:, n * TB:(n + 1) * TB, bs], bank[:, :, bs]

        spread_ids = slots[0:HOT_ROWS, :, :].rearrange("p s c -> p (s c)")
        ID_BANK = CH // P
        assert len(hot) <= 4 * ID_BANK

        block = ctx.enter_context(nc.Block())

        def gram_rows(dst, row, odd, g, j, r, bank):
            q0, q1 = ROUNDS[r]
            n, rows, fields = (q1 - q0) * QB, J, (F + 1 - odd) // 2
            cols = bass.ds(g * P + (j * (P // PAIRS) + q0 * QB), n)
            return (dst[J * odd:J * odd + rows, 0:fields, cols].rearrange("p i b -> p b i"),
                    bank[row:row + rows, 0:n * F].rearrange("p (b i) -> p b i", i=F)[:, :, odd:F:2])

        @block.sync
        def _(sp):
            sp.dma_start(ids_sb[:].rearrange("p (g f) -> p g f", g=GROUPS),
                         ids.rearrange("(g p) f -> p g f", p=P)).then_inc(ids_loaded, 16)
            sp.dma_start(id32[:], ident).then_inc(ident_loaded, 16)
            sp.dma_start(row_no[:], row_numbers.rearrange("p (c k) -> p c k", k=HOT_MAX)).then_inc(row_no_loaded, 16)
            for p in hot_pieces:
                for n, fs in hot_by_piece[p]:
                    for f in fs:
                        sp.dma_start(hot_table[p][:, hot_row0(p, f):hot_row0(p, f) + n, :],
                                      tables[f].rearrange("(p k) d -> p k d", p=HOT_ROWS)
                                      ).then_inc(hot_tables_loaded[p], 16)
            sp.dma_start(choice[:], choices.rearrange("p (m r) -> p m r", r=X3)).then_inc(choice_loaded, 16)
            for dst, src in ((w_pq, w1_pairs[0]), (w_qp, w1_pairs[1])):
                sp.dma_start(dst, src.rearrange("p (t j) -> p t j", j=J)).then_inc(wpair_loaded, 16)
            sp.wait_ge(wpair_made, 1)
            def shift_pair(g, j):
                k = g * PAIRS + j
                sp.wait_ge(a_copied, k + 1)
                for t in range(BY_PE, TILES):
                    for r in range(ROWS[t] // F):
                        s = PER_TILE * t + r
                        sp.dma_start(xb[F * r:F * (r + 1), j % 2, t - BY_PE, :],
                                     xa[s:s + F, j % 2, :]).then_inc(shifted[j % 2][t - BY_PE], 16)

            with sp.Fori(0, GROUPS) as g:
                for j in range(PAIRS):
                    shift_pair(g, j)
            sp.wait_ge(y_copied, 1)
            sp.dma_start(out.rearrange("b o -> o b"), y_sb[:]).then_inc(out_stored, 16)
            sp.wait_ge(out_stored, 16)

        TOP_LOADS = 8
        CIN_PIECES = 4
        CIN_LOADS = CIN_PIECES + 2
        WPAIR_LOADS = 2

        @block.gpsimd
        def _(gp):
            def gather_piece(p, ids_of_group, but=()):
                for f in [f for f in range(CUTS[p], CUTS[p + 1]) if f not in but]:
                    gp.indirect_dma_start(
                        out=emb[:, f, :], out_offset=None, in_=tables[f],
                        in_offset=bass.IndirectOffsetOnAxis(ap=ids_of_group[:, f:f + 1].bitcast(U32), axis=0),
                    ).then_inc(gathered[p], 16)

            gp.wait_ge(ids_loaded, 16)
            for p in range(PIECES):
                gather_piece(p, ids_sb, but=hot)
            with gp.Fori(1, GROUPS) as g:
                for p in range(PIECES):
                    gp.wait_ge(rest_made, PIECES * g + (p + 1 - PIECES))
                    gp.tensor_copy(idx[:, CUTS[p]:CUTS[p + 1]],
                                   ids_sb[:, bass.ds(g * F + CUTS[p], CUTS[p + 1] - CUTS[p])]).then_inc(idx_ready, 1)
                    gp.wait_ge(idx_ready, PIECES * g + (p + 1 - PIECES))
                    gp.sem_inc(idx_seen, 1)
                    gather_piece(p, idx)

            def pair_multiplied(k):
                gp.wait_ge(z_made[TILES - 1], k + 1)

            w2_rows = w2.rearrange("(i j) k -> j i k", j=J)
            w1_rows = w1[:, J:K1].rearrange("(i p) k -> p i k", p=F)
            gp.wait_ge(cin_zeros, 1)
            for i0 in range(0, F2, F2 // 2):
                pair_multiplied((GROUPS - 1) * PAIRS - 3 + 2 * i0 // F2)
                for odd in range(2):
                    n = min(F2 // 2, (F + 1 - odd) // 2 - i0)
                    gp.dma_start(w_c2[J * odd:J * (odd + 1), i0:i0 + n, :],
                                 w2_rows[:, 2 * i0 + odd:2 * (i0 + n) - 1 + odd:2, :]).then_inc(wcin_loaded, 16)
            gp.wait_ge(a_chosen, (GROUPS - 1) * PAIRS + 1)
            gp.memset(w_f1[:, :, :], 0.0).then_inc(late_zeros, 1)
            gp.dma_start(dense_sb[:], dense.rearrange("(g p) c -> p g c", p=P)).then_inc(top_loaded, 16)
            gp.wait_ge(rest_made, PIECES * GROUPS)
            gp.dma_start(w_t2, w_top2.rearrange("(c p) m -> p c m", p=P)).then_inc(top_loaded, 16)
            with nc.allow_non_contiguous_dma(reason="a few hundred biases and weights, one per partition"):
                gp.dma_start(w_t3[:], w_top3.rearrange("(c p) o -> p (c o)", p=P)).then_inc(top_loaded, 16)
                gp.dma_start(bias1[:], b_top1.rearrange("(c p) -> p c", p=P)).then_inc(top_loaded, 16)
                gp.dma_start(bias2[:], b_top2.rearrange("(c p) -> p c", p=P)).then_inc(top_loaded, 16)
            gp.dma_start(w_t1a[0:J, :], w_top1[0:J, :]).then_inc(top_loaded, 16)
            gp.dma_start(w_t1a[J:J + DENSE, :], w_top1[J + K2:J + K2 + DENSE, :]).then_inc(top_loaded, 16)
            gp.wait_ge(part3_made, PIECES * GROUPS)
            gp.dma_start(w_t1b, w_top1[J:J + K2, :]).then_inc(top_loaded, 16)
            gp.wait_ge(late_zeros, 1)
            for odd in range(2):
                pair_multiplied((GROUPS - 1) * PAIRS + odd)
                gp.dma_start(w_f1[J * odd:J * odd + F, 0:(F + 1 - odd) // 2, :],
                             w1_rows[:, odd:F:2, :]).then_inc(wcin_loaded, 16)

        @block.tensor
        def _(pe):
            def turn_batch(n, where):
                bank = where[0:X3, :].bitcast(BF16)
                for e in range(TB):
                    mm = pe.transpose(bank[:, e * P:(e + 1) * P], parts[:, n * TB + e, :], id16[:, :])
                mm.then_inc(turned, 1)

            def choose(g, j, which, slot, signal):
                rows = X3 if which == 0 else ROWS[which - 1]
                for c in range(2):
                    mm = pe.matmul(slots[0:rows, slot, c * CH:(c + 1) * CH], choice[:, which, 0:rows],
                                   xt[:, bass.ds(xt_base(g) + (j * COLS + c * CH), CH)], start=True, stop=True)
                mm.then_inc(signal, 1)

            def sum_tile(k, j, t, first):
                if t == 0 and not first:
                    pe.wait_ge(h_copied, k)
                for c in range(2):
                    mm = pe.matmul(ps_h[c * J:(c + 1) * J, :], w_pair[0:ROWS[t], t, :],
                                   z[0:ROWS[t], (TILES * j + t) % NZ, c * CH:(c + 1) * CH],
                                   start=(t == 0), stop=(t == TILES - 1))
                mm.then_inc(summed, 1)

            def turn_h(kp):
                pe.wait_ge(h_copied, kp + 1)
                pe.wait_ge(hx_copied, kp + 1)
                for q in range(CH // P):
                    mm = pe.transpose(ps_t[:, q * P:(q + 1) * P], h_sb[:, q * P:(q + 1) * P], id32[:, :])
                mm.then_inc(h_turned, 1)

            def turn_x(g, j):
                for q in range(QUADS):
                    mm = pe.matmul(ps_x[:, q * F:(q + 1) * F],
                                   xt[:, bass.ds(xt_base(g) + (j * COLS + q * P), P)],
                                   choice[:, 0, 0:F], start=True, stop=True)
                mm.then_inc(x_turned, 1)

            def gram_round(kp, par, r, bank=ps_g):
                if r == 0:
                    pe.wait_ge(hx_copied, kp + 2)
                    pe.wait_ge(x_copied, kp + 1)
                if bank is ps_g:
                    pe.wait_ge(g_copied, len(ROUNDS) * kp + r + 1)
                    pe.wait_ge(x_rows_copied, len(ROUNDS) * kp + r + 1)
                q0, q1 = ROUNDS[r]
                for q in range(q0, q1):
                    mm = pe.matmul(bank[:, (q - q0) * QB * F:(q - q0 + 1) * QB * F], hx[:, par, q, :],
                                   xdiag[:, par, q, :], start=True, stop=True)
                mm.then_inc(gram_done, 1)

            def sum_final1(i0, i1, b0, b1):
                for i in range(i0, i1):
                    half = slice(J * (i % 2), J * (i % 2 + 1))
                    mm = pe.matmul(slots[half, 0, B + b0:B + b1], w_f1[:, i, :], gram_x[0:HX, i, b0:b1],
                                   start=(i < 2), stop=(i >= F2 - 2))
                return mm

            BL = B - 2 * (P // PAIRS)
            FINAL1_CUTS = [2, 4, 10]

            def chunk_pair(g, j, first=False, last=False):
                k = g * PAIRS + j
                turns = j == PAIRS - 1 and not last
                gn, jn = (g + 1, 0) if j == PAIRS - 1 else (g, j + 1)
                for t in range(TILES):
                    pe.wait_ge(z_made[t], k + 1)
                    if t + 2 < BY_PE:
                        choose(g, j, t + 3, slot_of(j, t + 2), b_chosen)
                    if t == 2 and not last and not turns:
                        choose(gn, jn, 0, slot_of(j, BY_PE), a_chosen)
                    if t == 5 and not last:
                        choose(gn, jn, 1, slot_of(j + 1, 0), b_chosen)
                    sum_tile(k, j, t, first)
                    if t == 0 and not first:
                        turn_h(k - 1)
                    if turns and t == 1:
                        pe.wait_ge(part3_made, PIECES * (g + 2))
                        pe.wait_ge(x_copied, k + 1)
                        turn_batch(0, ps_x)
                    if turns and t == 2:
                        pe.wait_ge(hx_copied, k + 1)
                        turn_batch(1, ps_t)
                        pe.wait_ge(turned_copied, BATCHES * (g + 1) + 1)
                        turn_batch(2, ps_x)
                    if turns and t == 3:
                        pe.wait_ge(turned_copied, BATCHES * (g + 1) + 2)
                        turn_batch(3, ps_t)
                    if turns and t == 4:
                        pe.wait_ge(turned_copied, BATCHES * (g + 2))
                        choose(gn, jn, 0, slot_of(j, BY_PE), a_chosen)
                    if t == 6 and not last:
                        pe.wait_ge(a_copied, k + 2)
                        choose(gn, jn, 2, slot_of(j + 1, 1), b_chosen)
                        pe.wait_ge(x_copied, k + 1)
                        turn_x(gn, jn)
                    if t == 6 and last:
                        pe.wait_ge(wcin_loaded, 16 * CIN_LOADS)
                        pe.wait_ge(x_rows_copied, len(ROUNDS) * (k - 1) + 1)
                        sum_final1(0, FINAL1_CUTS[0], 0, BL)
                    if t in GRAM_STEPS and not first:
                        gram_round(k - 1, (j - 1) % 2, GRAM_STEPS.index(t))

            pe.wait_ge(ident_loaded, 16)
            pe.wait_ge(ids_f_made, 1)
            for c, f in enumerate(hot):
                pe.matmul(spread_ids[:, c * P:(c + 1) * P], ids_f[:, f:f + 1].to_broadcast([P, HOT_ROWS]),
                          id32[:, :], start=True, stop=True).then_inc(ids_spread, 1)
            for step, (p, n, k, fs, onehot) in enumerate(hot_steps):
                pe.wait_ge(hot_made, step + 1)
                first_step = step == 0 or hot_steps[step - 1][0] != p
                last_step = step + 1 == len(hot_steps) or hot_steps[step + 1][0] != p
                if first_step:
                    pe.wait_ge(hot_part3_made, hot_pieces.index(p) + 1)
                for c, f in enumerate(fs):
                    mm = pe.matmul(hot_place(p, f), onehot[:, c, :], hot_parts[p][:, hot_row0(p, f) + k, :, :],
                                   start=(first_step and c == 0), stop=(last_step and c == len(fs) - 1))
                if last_step:
                    mm.then_inc(hot_summed[p], 1)
            pe.wait_ge(choice_loaded, 16)
            pe.wait_ge(part3_made, 1)
            with pe.Fori(0, WARM_UPS) as _i:
                for c in range(2):
                    pe.matmul(ps_x[0:X3, 0:4 * X3], choice[:, 0, :],
                              choice[:, c * 4:c * 4 + 4, :], start=True, stop=True)
            pe.wait_ge(id16_made, 1)
            pe.wait_ge(part3_made, PIECES)
            for n in range(BATCHES):
                turn_batch(n, FIRST_BANKS[n])
            pe.wait_ge(first_copied, BATCHES)
            choose(0, 0, 0, slot_of(-1, BY_PE), a_chosen)
            choose(0, 0, 1, slot_of(0, 0), b_chosen)
            pe.wait_ge(a_copied, 1)
            choose(0, 0, 2, slot_of(0, 1), b_chosen)
            pe.wait_ge(turned_copied, BATCHES)
            turn_x(0, 0)
            pe.wait_ge(wpair_made, 1)
            chunk_pair(0, 0, first=True)
            with pe.Fori(0, GROUPS - 1) as g:
                for j in range(1, PAIRS):
                    chunk_pair(g, j)
                chunk_pair(g + 1, 0)
            for j in range(1, PAIRS):
                chunk_pair(GROUPS - 1, j, last=(j == PAIRS - 1))
            kl = GROUPS * PAIRS - 1
            pe.wait_ge(top_loaded, 16 * TOP_LOADS)
            for g in range(GROUPS):
                mm = pe.transpose(ps_dense[:, g * P:(g + 1) * P], dense_sb[:, g, :], id32[:, :])
            mm.then_inc(dense_turned, 1)

            sum_final1(FINAL1_CUTS[0], FINAL1_CUTS[1], 0, BL)
            turn_h(kl)
            sum_final1(FINAL1_CUTS[1], FINAL1_CUTS[2], 0, BL)
            for r in range(len(ROUNDS)):
                gram_round(kl, kl % 2, r, LAST_BANKS[r])
            sum_final1(FINAL1_CUTS[2], F2, 0, BL)
            pe.wait_ge(x_rows_copied, len(ROUNDS) * (kl + 1) + 1)
            sum_final1(0, F2, BL, B).then_inc(final1_done, 1)
            pe.wait_ge(g_copied, len(ROUNDS) * (kl + 1) + 1)
            for i in range(F2):
                mm = pe.matmul(slots[:, 0, 0:B], w_c2[:, i, :], gram_g[:, i, :], start=(i == 0), stop=(i == F2 - 1))
            mm.then_inc(conv2_done, 1)
            pe.wait_ge(dense_copied, 1)
            pe.wait_ge(final1_added, 1)
            top1_banks = [slots[:, 1, 0:B], slots[:, 1, B:2 * B], ps_h[:, :], ps_t[:, :]]
            for m in range(M1 // P):
                pe.matmul(top1_banks[m], w_t1a[:, m * P:(m + 1) * P], za[:, :], start=True, stop=False)
            pe.wait_ge(conv2_copied, 1)
            for m in range(M1 // P):
                pe.matmul(top1_banks[m], w_t1b[:, m * P:(m + 1) * P], conv2[:, :],
                          start=False, stop=True).then_inc(top1_done, 1)
            top2_banks = [ps_x[:, :], ps_g[:, :]]
            for c in range(M1 // P):
                if c % 2 == 0:
                    pe.wait_ge(top1_act, c // 2 + 1)
                else:
                    pe.wait_ge(top1_dve, c // 2 + 1)
                for m in range(M2 // P):
                    mm = pe.matmul(top2_banks[m], w_t2[:, c, m * P:(m + 1) * P], top1[:, c, :],
                                   start=(c == 0), stop=(c == M1 // P - 1))
                    if c == M1 // P - 1:
                        mm.then_inc(top2_done, 1)
            pe.wait_ge(top2_act, 1)
            pe.matmul(slots[0:1, 0, 0:B], w_t3[:, 0:1], top2[:, 0, :], start=True, stop=False)
            pe.wait_ge(top2_dve, 1)
            pe.matmul(slots[0:1, 0, 0:B], w_t3[:, 1:2], top2[:, 1, :], start=False, stop=True).then_inc(y_done, 1)

        @block.scalar
        def _(act):
            def part1(g, p):
                act.wait_ge(gathered[p], 16 * (CUTS[p + 1] - CUTS[p]) * g + 16 * gathers0[p])
                fs = slice(CUTS[p], CUTS[p + 1])
                act.copy(parts[:, :, CUTS[p]:CUTS[p + 1]].rearrange("p d f -> p f d"),
                         emb[:, fs, :]).then_inc(part1_made, 1)

            def part2(g, p):
                act.wait_ge(rest_made, PIECES * g + (p + 1))
                act.copy(parts[:, :, F + CUTS[p]:F + CUTS[p + 1]].rearrange("p d f -> p f d"),
                         rest[:, CUTS[p]:CUTS[p + 1], :]).then_inc(part2_made, 1)

            def copy_turned(g, n, where):
                act.wait_ge(turned, BATCHES * g + (n + 1))
                bank = where[0:X3, :].bitcast(BF16)
                dst = xt[:, bass.ds(xt_base(g), P * D)].rearrange("p (b d) -> p d b", d=D)
                act.copy(dst[:, n * TB:(n + 1) * TB, :],
                         bank.rearrange("p (e b) -> p e b", e=TB)).then_inc(turned_copied, 1)

            def copy_turned_first(n, signal):
                act.wait_ge(turned, n + 1)
                act.copy(*first_turned(n, signal is first_copied)).then_inc(signal, 1)

            def copy_a(k, j):
                act.wait_ge(a_chosen, k + 1)
                act.copy(xa[:, j % 2, :], slots[0:X3, slot_of(j - 1, BY_PE), :]).then_inc(a_copied, 1)

            def copy_h(kp):
                act.wait_ge(summed, TILES * (kp + 1))
                act.copy(h_sb[:, :], ps_h[:, :]).then_inc(h_copied, 1)

            def copy_hx(kp, par):
                act.wait_ge(h_turned, kp + 1)
                act.copy(hx[:, par, :, 0:J].rearrange("p (c q) m -> p q c m", c=2),
                         ps_t[:, :].rearrange("p (q c m) -> p q c m", c=2, m=J)).then_inc(hx_copied, 1)

            def copy_x(k, par):
                act.wait_ge(x_turned, k + 1)
                src = ps_x[:, 0:QUADS * F].rearrange("p (q f) -> p q f", f=F)
                act.copy(hx[:, par, :, J:HX], src)
                for y in range(QB):
                    rows = slice(y * D, (y + 1) * D)
                    op = act.copy(xdiag[rows, par, :, y * F:(y + 1) * F], src[rows])
                op.then_inc(x_copied, 1)

            def copy_g(gp_, jp, r, bank=ps_g):
                kp = gp_ * PAIRS + jp
                act.wait_ge(gram_done, len(ROUNDS) * kp + (r + 1))
                act.copy(*gram_rows(gram_g, 0, 0, gp_, jp, r, bank))
                act.copy(*gram_rows(gram_g, 0, 1, gp_, jp, r, bank)).then_inc(g_copied, 1)
                if r > 0:
                    act.copy(*gram_rows(gram_x, J, 0, gp_, jp, r, bank))
                    act.copy(*gram_rows(gram_x, J, 1, gp_, jp, r, bank)).then_inc(x_rows_copied, 1)

            def chunk_pair(g, j, first=False, last=False):
                k = g * PAIRS + j
                gp_, jp = (g, j - 1) if j else (g - 1, PAIRS - 1)
                splits = not (isinstance(g, int) and g == GROUPS - 1)
                if splits and j == 1:
                    part1(g + 1, 0)
                if splits and j == 2:
                    part1(g + 1, 1)
                copy_x(k, j % 2)
                if not first:
                    copy_hx(k - 1, jp % 2)
                if splits and j == PAIRS - 1:
                    for n in range(BATCHES):
                        copy_turned(g + 1, n, (ps_x, ps_t)[n % 2])
                if j < PAIRS - 1:
                    copy_a(k + 1, j + 1)
                if splits and j == 1:
                    part2(g + 1, 0)
                if splits and j == 2:
                    part2(g + 1, 1)
                if not first:
                    copy_g(gp_, jp, 0)
                if splits and j == 2:
                    part1(g + 1, 2)
                if j == PAIRS - 1 and not last:
                    copy_a(k + 1, j + 1)
                if not first:
                    copy_g(gp_, jp, 1)
                if splits and j == 2:
                    part2(g + 1, 2)
                copy_h(k)
                if not first:
                    copy_g(gp_, jp, 2)

            act.sem_inc(hx_copied, 1)
            act.sem_inc(g_copied, 1)
            act.sem_inc(x_rows_copied, 1)
            for c0 in range(0, len(hot), ID_BANK):
                c1 = min(len(hot), c0 + ID_BANK)
                act.wait_ge(ids_spread, c1)
                act.copy(id_cols[:, c0 * P:c1 * P], spread_ids[:, c0 * P:c1 * P]).then_inc(ids_copied, 1)
            act.wait_ge(ident_loaded, 16)
            act.copy(id16[:, :], id32[:, :]).then_inc(id16_made, 1)
            def hot_part1(c):
                p = hot_pieces[c]
                act.wait_ge(hot_tables_loaded[p], 16 * sum(len(fs) for _, fs in hot_by_piece[p]))
                act.copy(hot_parts[p][:, :, 0, :], hot_table[p]).then_inc(hot_part1_made, 1)

            def hot_part2(c):
                p = hot_pieces[c]
                act.wait_ge(hot_rest_made, c + 1)
                act.copy(hot_parts[p][:, :, 1, :], hot_table[p]).then_inc(hot_part2_made, 1)

            hot_part1(0)
            for c in range(1, len(hot_pieces)):
                hot_part1(c)
                hot_part2(c - 1)
            hot_part2(len(hot_pieces) - 1)
            act.wait_ge(hx_zeros, 1)
            for c in range(0, QB * F, P - HX):
                n = min(P - HX, QB * F - c)
                act.copy(xdiag[:, :, :, c:c + n], hx[:, :, :, HX:HX + n])
            for p in range(PIECES):
                if p in hot_pieces:
                    act.wait_ge(looked_up, hot_runs_until(p))
                part1(0, p)
                part2(0, p)
            for n in range(0, BATCHES, 2):
                copy_turned_first(n, first_copied)
            copy_a(0, 0)
            for n in range(0, BATCHES, 2):
                copy_turned_first(n, turned_copied)
            chunk_pair(0, 0, first=True)
            with act.Fori(0, GROUPS - 1) as g:
                for j in range(1, PAIRS):
                    chunk_pair(g, j)
                chunk_pair(g + 1, 0)
            for j in range(1, PAIRS):
                chunk_pair(GROUPS - 1, j, last=(j == PAIRS - 1))
            kl = GROUPS * PAIRS - 1
            act.wait_ge(dense_turned, 1)
            act.copy(za[J:J + DENSE, :], ps_dense).then_inc(dense_copied, 1)
            copy_hx(kl, kl % 2)
            for r in range(len(ROUNDS)):
                copy_g(GROUPS - 1, PAIRS - 1, r, LAST_BANKS[r])

            act.wait_ge(final1_done, 1)
            act.copy(f1_odd[:, :], slots[J:2 * J, 0, B:2 * B]).then_inc(final1_half, 1)
            act.wait_ge(conv2_done, 1)
            act.copy(conv2[:, :], slots[:, 0, 0:B]).then_inc(conv2_copied, 1)
            top1_banks = [slots[:, 1, 0:B], slots[:, 1, B:2 * B], ps_h[:, :], ps_t[:, :]]
            for m in range(0, M1 // P, 2):
                act.wait_ge(top1_done, m + 1)
                act.activation(top1[:, m, :], top1_banks[m], ACT.Relu, bias=bias1[:, m:m + 1]).then_inc(top1_act, 1)
            act.wait_ge(top2_done, 1)
            act.activation(top2[:, 0, :], ps_x[:, :], ACT.Relu, bias=bias2[:, 0:1]).then_inc(top2_act, 1)

        @block.vector
        def _(dv):
            def make_rest(g, p):
                dv.wait_ge(part1_made, PIECES * g + (p + 1))
                fs = slice(CUTS[p], CUTS[p + 1])
                dv.tensor_tensor(rest[:, fs, :], emb[:, fs, :],
                                 parts[:, :, CUTS[p]:CUTS[p + 1]].rearrange("p d f -> p f d"),
                                 ALU.subtract).then_inc(rest_made, 1)

            def part3(g, p):
                dv.wait_ge(part2_made, PIECES * g + (p + 1))
                dv.tensor_tensor(parts[:, :, 2 * F + CUTS[p]:2 * F + CUTS[p + 1]].rearrange("p d f -> p f d"),
                                 rest[:, CUTS[p]:CUTS[p + 1], :],
                                 parts[:, :, F + CUTS[p]:F + CUTS[p + 1]].rearrange("p d f -> p f d"),
                                 ALU.subtract).then_inc(part3_made, 1)

            def make_z(k, g, j, t, first):
                if t == 0:
                    dv.wait_ge(a_copied, k + 1)
                n = ROWS[t]
                if t >= NZ or (t >= BY_PE and not first):
                    dv.wait_ge(summed, TILES * k + (t - NZ + 1))
                if t < BY_PE:
                    dv.wait_ge(b_chosen, BY_PE * k + (t + 1))
                    b_rows = slots[0:n, slot_of(j, t), :]
                else:
                    dv.wait_ge(shifted[j % 2][t - BY_PE], 16 * (n // F) * (PAIRS // 2 * g + (j // 2 + 1)))
                    b_rows = xb[0:n, j % 2, t - BY_PE, :]
                dv.tensor_tensor(z[0:n, (TILES * j + t) % NZ, :], xa[0:n, j % 2, :], b_rows,
                                 ALU.mult).then_inc(z_made[t], 1)

            def copy_turned_first(n, signal):
                dv.wait_ge(turned, n + 1)
                dv.tensor_copy(*first_turned(n, signal is first_copied)).then_inc(signal, 1)

            def copy_x_rows(g, j, r, bank=ps_g):
                dv.wait_ge(gram_done, len(ROUNDS) * (g * PAIRS + j) + (r + 1))
                dv.tensor_copy(*gram_rows(gram_x, J, 0, g, j, r, bank))
                dv.tensor_copy(*gram_rows(gram_x, J, 1, g, j, r, bank)).then_inc(x_rows_copied, 1)

            def chunk_pair(g, j, first=False):
                k = g * PAIRS + j
                gp_, jp = (g, j - 1) if j else (g - 1, PAIRS - 1)
                splits = not (isinstance(g, int) and g == GROUPS - 1)
                for t in range(TILES):
                    make_z(k, g, j, t, first)
                    if t == 5 and not first:
                        copy_x_rows(gp_, jp, 0)
                    if splits and j == 1:
                        if t == 2:
                            make_rest(g + 1, 0)
                        if t == 5:
                            part3(g + 1, 0)
                    if splits and j == 2:
                        if t == 2:
                            make_rest(g + 1, 1)
                        if t == 5:
                            part3(g + 1, 1)
                        if t == 6:
                            make_rest(g + 1, 2)
                    if splits and j == 3:
                        if t == 0:
                            part3(g + 1, 2)

            dv.memset(w_c2[J:2 * J, F2 - 1, :], 0.0).then_inc(cin_zeros, 1)
            dv.memset(gram_g[J:2 * J, F2 - 1, :], 0.0)
            dv.memset(gram_x[J:2 * J, F2 - 1, :], 0.0)
            dv.memset(hx[:, :, :, HX:P], 0.0).then_inc(hx_zeros, 1)
            dv.wait_ge(ids_loaded, 16)
            dv.tensor_copy(ids_f[:, :], ids_sb[:, 0:F]).then_inc(ids_f_made, 1)
            dv.wait_ge(row_no_loaded, 16)

            def one_hots(piece):
                for p, n, k, fs, onehot in hot_steps:
                    if p != piece:
                        continue
                    c0 = hot.index(fs[0])
                    dv.wait_ge(ids_copied, -(-(c0 + len(fs)) // ID_BANK))
                    c_n = hot_counts.index(n)
                    dv.tensor_scalar(onehot, id_cols[:, c0 * P:(c0 + len(fs)) * P].rearrange(
                        "p (f b) -> p f b", b=P), row_no[:, c_n, k:k + 1], None, ALU.is_equal).then_inc(hot_made, 1)

            def hot_make_rest(c):
                p = hot_pieces[c]
                dv.wait_ge(hot_part1_made, c + 1)
                dv.tensor_tensor(hot_table[p], hot_table[p], hot_parts[p][:, :, 0, :],
                                 ALU.subtract).then_inc(hot_rest_made, 1)

            def hot_part3(c):
                p = hot_pieces[c]
                dv.wait_ge(hot_part2_made, c + 1)
                dv.tensor_tensor(hot_parts[p][:, :, 2, :], hot_table[p], hot_parts[p][:, :, 1, :],
                                 ALU.subtract).then_inc(hot_part3_made, 1)

            def put_looked_up(p):
                dv.wait_ge(hot_summed[p], 1)
                for f0, count, c in runs_of([f for _, fs in hot_by_piece[p] for f in fs]):
                    dv.tensor_reduce(emb[:, f0:f0 + count, :],
                                     HOT_BANKS[p][:, c * 3 * D:(c + count) * 3 * D].rearrange(
                                         "p (f t d) -> p f d t", t=3, d=D),
                                     AXES.X, ALU.add).then_inc(looked_up, 1)

            one_hots(hot_pieces[0])
            for c in range(1, len(hot_pieces)):
                one_hots(hot_pieces[c])
                hot_make_rest(c - 1)
                if c > 1:
                    hot_part3(c - 2)
            hot_make_rest(len(hot_pieces) - 1)
            hot_part3(len(hot_pieces) - 2)
            hot_part3(len(hot_pieces) - 1)
            for p in range(PIECES):
                if p in hot_pieces:
                    put_looked_up(p)
                make_rest(0, p)
                part3(0, p)
                if p == 0:
                    dv.wait_ge(wpair_loaded, 16 * WPAIR_LOADS)
                    dv.tensor_tensor(w_pair[:, 0:TILES - 1, :], w_pq[:, 0:TILES - 1, :], w_qp[:, 0:TILES - 1, :], ALU.add)
                    dv.tensor_tensor(w_pair[0:ROWS[-1], TILES - 1, :], w_pq[0:ROWS[-1], TILES - 1, :],
                                     w_qp[0:ROWS[-1], TILES - 1, :], ALU.add).then_inc(wpair_made, 1)
            for signal in (first_copied, turned_copied):
                for n in range(1, BATCHES, 2):
                    copy_turned_first(n, signal)
            chunk_pair(0, 0, first=True)
            with dv.Fori(0, GROUPS - 1) as g:
                for j in range(1, PAIRS):
                    chunk_pair(g, j)
                chunk_pair(g + 1, 0)
            for j in range(1, PAIRS):
                chunk_pair(GROUPS - 1, j)

            copy_x_rows(GROUPS - 1, PAIRS - 1, 0, LAST_BANKS[0])
            dv.wait_ge(final1_half, 1)
            dv.tensor_tensor(za[0:J, :], slots[0:J, 0, B:2 * B], f1_odd[:, :], ALU.add).then_inc(final1_added, 1)
            top1_banks = [slots[:, 1, 0:B], slots[:, 1, B:2 * B], ps_h[:, :], ps_t[:, :]]
            for m in range(1, M1 // P, 2):
                dv.wait_ge(top1_done, m + 1)
                dv.tensor_scalar(top1[:, m, :], top1_banks[m], bias1[:, m:m + 1], 0.0, ALU.add,
                                 ALU.max).then_inc(top1_dve, 1)
            dv.wait_ge(top2_done, 2)
            dv.tensor_scalar(top2[:, 1, :], ps_g[:, :], bias2[:, 1:2], 0.0, ALU.add, ALU.max).then_inc(top2_dve, 1)
            dv.wait_ge(y_done, 1)
            dv.tensor_copy(y_sb[:, :], slots[0:1, 0, 0:B]).then_inc(y_copied, 1)


TABLES = [f"tbl_{f}" for f in range(F)]
OTHERS = ["dense_ctx", "ids", "W_top1", "b_top1", "W_top2", "b_top2", "W_top3", "L0_rec_W1", "L0_rec_W2"]


def table_rows(counts):
    m = np.full((HOT_ROWS, len(counts), HOT_MAX), -1, np.float32)
    for c, n in enumerate(counts):
        m[:, c, :n] = np.arange(HOT_ROWS)[:, None] * n + np.arange(n)
    return m.reshape(HOT_ROWS, len(counts) * HOT_MAX)


def kernel(**inputs):
    import ml_dtypes
    import concourse.bacc as bacc
    from concourse.bass_utils import run_bass_kernel_spmd

    nc = bacc.Bacc("TRN2", target_bir_lowering=False, num_devices=1)
    arrays, ap = {}, {}

    def give(name, a):
        arrays[name] = a
        ap[name] = nc.dram_tensor(name, a.shape, mybir.dt.from_np(a.dtype), kind="ExternalInput").ap()

    for name in TABLES + OTHERS:
        give(name, np.ascontiguousarray(inputs[name]))
    give("choices", field_choices().astype(ml_dtypes.bfloat16))
    give("ident", np.eye(P, dtype=np.float32))
    by_piece, _ = hot_fields([inputs[t].shape[0] for t in TABLES])
    give("w1_pairs", by_pairs(inputs["L0_rec_W1"]))
    give("row_numbers", table_rows(sorted({n for classes in by_piece for n, _ in classes})))
    out = nc.dram_tensor("y", (B, 1), F32, kind="ExternalOutput").ap()
    dlrm_tower(nc, ap["dense_ctx"], ap["ids"], [ap[t] for t in TABLES], ap["W_top1"], ap["b_top1"], ap["W_top2"],
               ap["b_top2"], ap["W_top3"], ap["L0_rec_W1"], ap["w1_pairs"],
               ap["L0_rec_W2"], ap["choices"], ap["ident"], ap["row_numbers"], out)
    r = run_bass_kernel_spmd(nc, [arrays], core_ids=[0])
    return r.results[0]["y"]
```
